# Optimizing a Trainium2 kernel written in Bass

```python
import numpy as np
import jax
import jax.numpy as jnp

def _softmax(x, axis=-1):
    return jax.nn.softmax(x, axis=axis)

def _gelu(x):
    return jax.nn.gelu(x, approximate=True)

def _silu(x):
    return jax.nn.silu(x)

def _sigmoid(x):
    return jax.nn.sigmoid(x)

def _layernorm(x, axis=-1, eps=1e-05):
    m = jnp.mean(x, axis=axis, keepdims=True)
    v = jnp.var(x, axis=axis, keepdims=True)
    return (x - m) / jnp.sqrt(v + eps)

def _scatter_add(tgt, idx, src, axis=0):
    return tgt.at[idx].add(src)

def _segment_sum(src, seg, n):
    return jax.ops.segment_sum(src, seg, n)
kernel_name = 'mk_xattn_seq_d1_seqx_r2_f6096f'

def setup_inputs(seed: int=0):
    np.random.seed(seed)
    _w = jnp.asarray

    def _rec_inputs():
        import jax
        import jax.numpy as jnp
        _rk = jax.random.key(seed)
        x = -0.000296 + 1 * jax.random.normal(jax.random.fold_in(_rk, 1), (8, 1024, 640), jnp.float32)
        _lenS = 1024 - jax.random.randint(jax.random.fold_in(_rk, 7), (8,), 0, max(1, 1024 // 4) + 1, jnp.int32)
        _lenS2 = 64 - jax.random.randint(jax.random.fold_in(_rk, 8), (8,), 0, max(1, 64 // 4) + 1, jnp.int32)
        _ctx_2048P = jax.random.normal(jax.random.fold_in(_rk, 11), (8, 16, 1024), jnp.float32)
        _ctx_2048c = jax.random.dirichlet(jax.random.fold_in(_rk, 511), 0.3 * jnp.ones((16,), jnp.float32), (8, 64))
        _ctx_2048t = jnp.einsum('bsk,bkd->bsd', _ctx_2048c, _ctx_2048P)
        _ctx_2048t = _ctx_2048t * jax.lax.rsqrt(jnp.mean(jnp.square(_ctx_2048t)) + 1e-12) * 0.953939
        ctx_2048 = 0.00118529 + 0.99962 * (_ctx_2048t + 0.3 * jax.random.normal(jax.random.fold_in(_rk, 611), (8, 64, 1024), jnp.float32))
        fside_Bx4x4_0 = jax.random.uniform(jax.random.fold_in(_rk, 12), (8, 4, 4), jnp.float32, 0.0, 0.981965)
        return (x, ctx_2048, fside_Bx4x4_0)
    x, ctx_2048, fside_Bx4x4_0 = _rec_inputs()

    def _L0_xattn_setup():
        import jax, jax.numpy as jnp
        import numpy as np
        HEADS = 20
        NUM_IP_TOKENS = 4
        NUM_DUMMY_TOKENS = 4
        IP_SCALE = 1.0
        ASPECT_RATIO = 1.0
        NEG = -10000.0

        def _grid_hw(seq_len, aspect_ratio):
            width = int((seq_len / aspect_ratio) ** 0.5)
            height = seq_len // width
            while width * height != seq_len:
                if width * height < seq_len:
                    width += 1
                else:
                    width -= 1
                height = seq_len // width
            return (height, width)

        def _sdpa(q, k, v, mask=None):
            dh = q.shape[-1]
            scores = jnp.einsum('bhqd,bhkd->bhqk', q, k) / jnp.sqrt(jnp.asarray(dh, q.dtype))
            if mask is not None:
                scores = scores + mask
            probs = jax.nn.softmax(scores, axis=-1)
            return jnp.einsum('bhqk,bhkd->bhqd', probs, v)

        def _split_heads(x, heads):
            b, l, d = x.shape
            return x.reshape(b, l, heads, d // heads).transpose(0, 2, 1, 3)

        def _merge_heads(x):
            b, h, l, dh = x.shape
            return x.transpose(0, 2, 1, 3).reshape(b, l, h * dh)

        def _ip_mask(bbox, batch_size, seq_len, dtype):
            M = bbox.shape[1]
            height, width = _grid_hw(seq_len, ASPECT_RATIO)
            x = jnp.linspace(0.0, 1.0, width, dtype=dtype)
            y = jnp.linspace(0.0, 1.0, height, dtype=dtype)
            yg, xg = jnp.meshgrid(y, x, indexing='ij')
            xg = xg.reshape(-1)
            yg = yg.reshape(-1)
            x1, y1, x2, y2 = (bbox[..., 0:1], bbox[..., 1:2], bbox[..., 2:3], bbox[..., 3:4])
            inside = (xg >= x1) & (xg <= x2) & (yg >= y1) & (yg <= y2)
            ip_mask = jnp.where(inside, 0.0, NEG).astype(dtype)
            ip_mask = jnp.transpose(ip_mask, (0, 2, 1))[:, None]
            ip_mask = jnp.repeat(ip_mask, NUM_IP_TOKENS // M, axis=-1)
            dummy = jnp.where(jnp.any(inside, axis=1), NEG, 0.0).astype(dtype)
            dummy = jnp.repeat(dummy[:, None, :, None], NUM_DUMMY_TOKENS, axis=-1)
            return jnp.concatenate([dummy, ip_mask], axis=-1)
        key = jax.random.key(seed)
        ks = jax.random.split(key, 12)
        B, S, D, C = (4, 2048, 640, 1024)
        text_len, M = (77, 4)
        hidden_states = jax.random.normal(ks[0], (B, S, D), jnp.float32)
        encoder_hidden_states = jax.random.normal(ks[1], (B, text_len + NUM_IP_TOKENS + NUM_DUMMY_TOKENS, C), jnp.float32)
        p1 = jax.random.uniform(ks[2], (B, M, 2), jnp.float32)
        p2 = jax.random.uniform(ks[3], (B, M, 2), jnp.float32)
        bbox = jnp.concatenate([jnp.minimum(p1, p2), jnp.maximum(p1, p2)], axis=-1)
        s = 0.02
        w_q = jax.random.normal(ks[4], (D, D), jnp.float32) * s
        w_k = jax.random.normal(ks[5], (C, D), jnp.float32) * s
        w_v = jax.random.normal(ks[6], (C, D), jnp.float32) * s
        w_k_ip = jax.random.normal(ks[7], (C, D), jnp.float32) * s
        w_v_ip = jax.random.normal(ks[8], (C, D), jnp.float32) * s
        w_out = jax.random.normal(ks[9], (D, D), jnp.float32) * s
        b_out = jnp.zeros((D,), jnp.float32)
        return {'hidden_states': hidden_states, 'encoder_hidden_states': encoder_hidden_states, 'bbox': bbox, 'w_q': w_q, 'w_k': w_k, 'w_v': w_v, 'w_k_ip': w_k_ip, 'w_v_ip': w_v_ip, 'w_out': w_out, 'b_out': b_out}
    _L0_xattn_all = _L0_xattn_setup()
    _L0_xattn_in = {k: v for k, v in _L0_xattn_all.items() if k in ('w_q', 'w_k', 'w_v', 'w_k_ip', 'w_v_ip', 'w_out', 'b_out')}
    del _L0_xattn_all
    return {'x': x, 'ctx_2048': ctx_2048, 'fside_Bx4x4_0': fside_Bx4x4_0, 'L0_xattn_w_q': _L0_xattn_in['w_q'], 'L0_xattn_w_k': _L0_xattn_in['w_k'], 'L0_xattn_w_v': _L0_xattn_in['w_v'], 'L0_xattn_w_k_ip': _L0_xattn_in['w_k_ip'], 'L0_xattn_w_v_ip': _L0_xattn_in['w_v_ip'], 'L0_xattn_w_out': _L0_xattn_in['w_out'], 'L0_xattn_b_out': _L0_xattn_in['b_out']}

def reference(x, ctx_2048, fside_Bx4x4_0, L0_xattn_w_q, L0_xattn_w_k, L0_xattn_w_v, L0_xattn_w_k_ip, L0_xattn_w_v_ip, L0_xattn_w_out, L0_xattn_b_out):
    import jax
    import jax.numpy as jnp

    def _L0_xattn_ref(hidden_states, encoder_hidden_states, bbox, w_q, w_k, w_v, w_k_ip, w_v_ip, w_out, b_out):
        import jax, jax.numpy as jnp
        import numpy as np
        HEADS = 20
        NUM_IP_TOKENS = 4
        NUM_DUMMY_TOKENS = 4
        IP_SCALE = 1.0
        ASPECT_RATIO = 1.0
        NEG = -10000.0

        def _grid_hw(seq_len, aspect_ratio):
            width = int((seq_len / aspect_ratio) ** 0.5)
            height = seq_len // width
            while width * height != seq_len:
                if width * height < seq_len:
                    width += 1
                else:
                    width -= 1
                height = seq_len // width
            return (height, width)

        def _sdpa(q, k, v, mask=None):
            dh = q.shape[-1]
            scores = jnp.einsum('bhqd,bhkd->bhqk', q, k) / jnp.sqrt(jnp.asarray(dh, q.dtype))
            if mask is not None:
                scores = scores + mask
            probs = jax.nn.softmax(scores, axis=-1)
            return jnp.einsum('bhqk,bhkd->bhqd', probs, v)

        def _split_heads(x, heads):
            b, l, d = x.shape
            return x.reshape(b, l, heads, d // heads).transpose(0, 2, 1, 3)

        def _merge_heads(x):
            b, h, l, dh = x.shape
            return x.transpose(0, 2, 1, 3).reshape(b, l, h * dh)

        def _ip_mask(bbox, batch_size, seq_len, dtype):
            M = bbox.shape[1]
            height, width = _grid_hw(seq_len, ASPECT_RATIO)
            x = jnp.linspace(0.0, 1.0, width, dtype=dtype)
            y = jnp.linspace(0.0, 1.0, height, dtype=dtype)
            yg, xg = jnp.meshgrid(y, x, indexing='ij')
            xg = xg.reshape(-1)
            yg = yg.reshape(-1)
            x1, y1, x2, y2 = (bbox[..., 0:1], bbox[..., 1:2], bbox[..., 2:3], bbox[..., 3:4])
            inside = (xg >= x1) & (xg <= x2) & (yg >= y1) & (yg <= y2)
            ip_mask = jnp.where(inside, 0.0, NEG).astype(dtype)
            ip_mask = jnp.transpose(ip_mask, (0, 2, 1))[:, None]
            ip_mask = jnp.repeat(ip_mask, NUM_IP_TOKENS // M, axis=-1)
            dummy = jnp.where(jnp.any(inside, axis=1), NEG, 0.0).astype(dtype)
            dummy = jnp.repeat(dummy[:, None, :, None], NUM_DUMMY_TOKENS, axis=-1)
            return jnp.concatenate([dummy, ip_mask], axis=-1)
        B, S, D = hidden_states.shape
        residual = hidden_states
        end_pos = encoder_hidden_states.shape[1] - (NUM_IP_TOKENS + NUM_DUMMY_TOKENS)
        text = encoder_hidden_states[:, :end_pos]
        ip_h = encoder_hidden_states[:, end_pos:]
        q = _split_heads(hidden_states @ w_q, HEADS)
        k = _split_heads(text @ w_k, HEADS)
        v = _split_heads(text @ w_v, HEADS)
        out_text = _sdpa(q, k, v)
        out_text = _merge_heads(out_text)
        mask_ip = _ip_mask(bbox, B, S, hidden_states.dtype)
        k_ip = _split_heads(ip_h @ w_k_ip, HEADS)
        v_ip = _split_heads(ip_h @ w_v_ip, HEADS)
        out_ip = _merge_heads(_sdpa(q, k_ip, v_ip, mask=mask_ip))
        out = out_text + IP_SCALE * out_ip
        out = out @ w_out + b_out
        out = out + residual
        return out
    x = _L0_xattn_ref(x, ctx_2048, fside_Bx4x4_0, L0_xattn_w_q, L0_xattn_w_k, L0_xattn_w_v, L0_xattn_w_k_ip, L0_xattn_w_v_ip, L0_xattn_w_out, L0_xattn_b_out)
    return x

_drawn_inputs = setup_inputs


def setup_inputs(seed=0):
    import zlib

    import numpy as np

    out = dict(_drawn_inputs(seed))
    spreads = {'L0_xattn_b_out': (0.0, 0.1)}
    factors = {'L0_xattn_w_k': 2.785}
    for name, (base, spread) in spreads.items():
        noise = np.random.default_rng([zlib.crc32(name.encode()), seed]).standard_normal(out[name].shape)
        drawn = base * np.exp(spread * noise) if base else spread * noise
        out[name] = jnp.asarray(drawn.astype(out[name].dtype))
    for name, factor in factors.items():
        out[name] = (out[name] * factor).astype(out[name].dtype)
    return out
```

```python
from contextlib import ExitStack

import concourse.bass as bass
from concourse import mybir

F32 = mybir.dt.float32
F32R = mybir.dt.float32r
ACT = mybir.ActivationFunctionType
ALU = mybir.AluOpType
AX = mybir.AxisListType

P = 128
HEADS, DH = 20, 32
NIP = 8
BOXES = 4
NEG = -10000.0
GRID = 32
GQ = 512
GT = GQ // P
RING = 4


def attention_kernel(nc, x, ctx, bbox, w_q, w_k, w_v, w_k_ip, w_v_ip, w_out, b_out, grid_x, grid_y, out):
    B, S, D = x.shape
    KEYS, C = ctx.shape[1:]
    NTEXT = KEYS - NIP
    KD, KC = D // P, C // P
    NG = B * S // GQ
    GPB = S // GQ
    TPB = S // P
    HPT = P // DH
    PAIRS = HEADS // 2
    CW = HPT * KEYS
    SW = HEADS * KEYS
    UNITS = GT * SW // 512
    HALF = D // 2
    PB = 2 * NTEXT
    NPB = B // 2
    TT, TI = B * NTEXT, B * NIP
    SCALE = float(DH) ** -0.5

    x_g = x.rearrange("b (h t p) d -> (b h) p t d", t=GT, p=P)
    out_t = out.rearrange("b (h t p) d -> (b h) t p d", t=GT, p=P)
    k_scratch = nc.dram_tensor("k_scratch", (P, B, KD * KEYS), F32).ap()
    v_scratch = nc.dram_tensor("v_scratch", (B, KEYS, D), F32).ap()

    whole = ExitStack()
    with whole:
        def sb(name, shape, dt=F32, stack=whole):
            return stack.enter_context(nc.sbuf_tensor(name, shape, dt))

        def sem(name):
            return whole.enter_context(nc.semaphore(name))

        bank = [whole.enter_context(nc.psum_tensor(f"bank{i}", [P, 512], F32)) for i in range(8)]

        ident = sb("ident", [P, P])
        wq_hi, wq_lo = sb("wq_hi", [P, KD, D], F32R), sb("wq_lo", [P, KD, D], F32R)
        wo_hi, wo_lo = sb("wo_hi", [P, KD, D], F32R), sb("wo_lo", [P, KD, D], F32R)
        xin = sb("xin", [P, 2, GT, D])
        mask = sb("mask", [P, B * TPB, NIP])
        bias = sb("bias", [P, D])

        x_loaded = [sem("x_loaded0"), sem("x_loaded1")]
        small_loaded = sem("small_loaded")
        ident_zeroed, ident_made = sem("ident_zeroed"), sem("ident_made")

        setup = ExitStack()
        with setup:
            ctx_text = sb("ctx_text", [PB, NPB, C], F32, setup)
            ctx_ip = sb("ctx_ip", [TI, C], F32, setup)
            ctxT_hi = sb("ctxT_hi", [P, KC, TT + TI], F32R, setup)
            ctxT_lo = sb("ctxT_lo", [P, KC, TT + TI], F32R, setup)
            w_raw = sb("w_raw", [P, RING, D], F32, setup)
            w_hi = sb("w_hi", [P, RING, D], F32R, setup)
            w_lo = sb("w_lo", [P, RING, D], F32R, setup)
            k_all = sb("k_all", [P, B, KD, KEYS], F32, setup)
            k_ip = sb("k_ip", [P, D], F32, setup)
            v_text = sb("v_text", [PB, NPB, D], F32, setup)
            v_ip = sb("v_ip", [P, D], F32, setup)
            boxes = sb("boxes", [P, B * BOXES, 4], F32, setup)
            gx, gy = sb("gx", [P, 1], F32, setup), sb("gy", [P, TPB], F32, setup)
            in_x = sb("inside_x", [P, 2, B * BOXES], F32, setup)
            in_y = sb("inside_y", [P, 2, B * BOXES, TPB], F32, setup)
            inside = sb("inside", [P, B, BOXES, TPB], F32, setup)
            any_in = sb("any_in", [P, B, TPB], F32, setup)

            chunks = [(w, k) for w in (w_v, w_k, w_k_ip, w_v_ip) for k in range(KC)]
            KV_CHUNKS = len(chunks)
            chunks += [(w, k) for w in (w_q, w_out) for k in range(KD)]
            V0, K0, KI0, VI0 = (i * KC for i in range(4))
            WQ0, WO0 = KV_CHUNKS, KV_CHUNKS + KD

            def split_dst(c):
                if c < WQ0:
                    return w_hi[:, c % RING, :], w_lo[:, c % RING, :]
                if c < WO0:
                    return wq_hi[:, c - WQ0, :], wq_lo[:, c - WQ0, :]
                return wo_hi[:, c - WO0, :], wo_lo[:, c - WO0, :]

            ctx_loaded = sem("ctx_loaded")
            w_loaded = [sem(f"w_loaded{i}") for i in range(RING)]
            w_hi_done, w_lo_done, w_used = sem("w_hi_done"), sem("w_lo_done"), sem("w_used")
            ctxT_ready, ctxT_hi_done, ctxT_lo_done = sem("ctxT_ready"), sem("ctxT_hi_done"), sem("ctxT_lo_done")
            v_text_ready, k_text_ready = sem("v_text_ready"), sem("k_text_ready")
            k_ip_ready, v_ip_ready, k_ipT_ready = sem("k_ip_ready"), sem("v_ip_ready"), sem("k_ipT_ready")
            v_text_act, v_text_dve = sem("v_text_act"), sem("v_text_dve")
            k_text_act, k_text_dve = sem("k_text_act"), sem("k_text_dve")
            k_ip_act, k_ip_dve = sem("k_ip_act"), sem("k_ip_dve")
            v_ip_act, v_ip_dve, k_ipT_act = sem("v_ip_act"), sem("v_ip_dve"), sem("k_ipT_act")
            mask_step, scratch_stored = sem("mask_step"), sem("scratch_stored")

            with nc.Block() as block:

                @block.sync
                def _(sp):
                    pairs = ctx.rearrange("(i j) k c -> j k i c", j=2)
                    for j in range(2):
                        sp.dma_start(ctx_text[j * NTEXT:(j + 1) * NTEXT, :, :], pairs[j, 0:NTEXT, :, :]).then_inc(ctx_loaded, 16)
                    for b in range(B):
                        sp.dma_start(ctx_ip[b * NIP:(b + 1) * NIP, :], ctx[b, NTEXT:KEYS, :]).then_inc(ctx_loaded, 16)
                    for c, (w, k) in enumerate(chunks):
                        if c >= RING:
                            sp.wait_ge(w_lo_done, c - RING + 1)
                        sp.dma_start(w_raw[:, c % RING, :], w[k * P:(k + 1) * P, :]).then_inc(w_loaded[c % RING], 16)
                    v_pairs = v_scratch.rearrange("(i j) k d -> j k i d", j=2)
                    sp.wait_ge(v_text_act, NPB)
                    sp.wait_ge(v_text_dve, NPB)
                    for j in range(2):
                        sp.dma_start(v_pairs[j, 0:NTEXT, :, :], v_text[j * NTEXT:(j + 1) * NTEXT, :, :]).then_inc(scratch_stored, 16)
                    sp.wait_ge(v_ip_act, 1)
                    sp.wait_ge(v_ip_dve, 1)
                    for b in range(B):
                        sp.dma_start(v_scratch[b, NTEXT:KEYS, :], v_ip[P - TI + b * NIP:P - TI + (b + 1) * NIP, :]).then_inc(scratch_stored, 16)
                    sp.wait_ge(k_text_act, (KD + 1) // 2)
                    sp.wait_ge(k_text_dve, KD // 2)
                    sp.wait_ge(k_ipT_act, 2)
                    sp.dma_start(k_scratch.rearrange("p b n -> p (b n)"), k_all[:].rearrange("p b m k -> p (b m k)")).then_inc(scratch_stored, 16)
                    sp.wait_ge(scratch_stored, 16 * (3 + B))

                @block.gpsimd
                def _(pool):
                    nc.gpsimd.memset(ident[:], 0.0).then_inc(ident_zeroed, 1)
                    pool.wait_ge(ident_zeroed, 1)
                    nc.gpsimd.affine_select(out=ident[:], in_=ident[:], compare_op=ALU.not_equal, fill=1.0, base=0,
                                            pattern=[[-1, P]], channel_multiplier=1).then_inc(ident_made, 1)
                    for c in range(len(chunks)):
                        hi, lo = split_dst(c)
                        pool.wait_ge(w_hi_done, c + 1)
                        nc.gpsimd.tensor_tensor(lo, w_raw[:, c % RING, :], hi.bitcast(F32), ALU.subtract).then_inc(w_lo_done, 1)

                @block.scalar
                def _(act):
                    for u in range(2):
                        act.dma_start(xin[:, u, :, :], x_g[u]).then_inc(x_loaded[u], 16)
                    act.dma_start(bias[:], b_out.rearrange("(o d) -> o d", o=1).broadcast_to([P, D])).then_inc(small_loaded, 16)
                    act.dma_start(boxes[:].rearrange("p n f -> p (n f)"),
                                  bbox.rearrange("(o b) m f -> o (b m f)", o=1).broadcast_to([P, B * BOXES * 4])).then_inc(small_loaded, 16)
                    act.dma_start(gx[:], grid_x).then_inc(small_loaded, 16)
                    act.dma_start(gy[:], grid_y).then_inc(small_loaded, 16)

                    def round_chunk(c):
                        act.wait_ge(w_loaded[c % RING], 16 * (c // RING + 1))
                        if RING <= c < WQ0:
                            w, k = divmod(c - RING, KC)
                            if k == KC - 1:
                                act.wait_ge(*((v_text_ready, 2 * NPB), (k_text_ready, KD), (k_ip_ready, 2))[w])
                            else:
                                act.wait_ge(w_used, w * (KC - 1) + k + 1)
                        nc.scalar.activation(split_dst(c)[0], w_raw[:, c % RING, :], ACT.Copy).then_inc(w_hi_done, 1)

                    for k in range(KC):
                        act.wait_ge(ctxT_ready, k + 1)
                        nc.scalar.activation(ctxT_hi[:, k, :], bank[k][:], ACT.Copy).then_inc(ctxT_hi_done, 1)
                    for c in range(V0, K0 + RING):
                        round_chunk(c)
                    for i in range(NPB):
                        act.wait_ge(v_text_ready, 2 * i + 1)
                        nc.scalar.activation(v_text[:, i, 0:HALF], bank[2 * i][0:PB, 0:HALF], ACT.Copy).then_inc(v_text_act, 1)
                    for c in range(K0 + RING, KI0 + RING):
                        round_chunk(c)
                    for m in range(0, KD, 2):
                        act.wait_ge(k_text_ready, m + 1)
                        nc.scalar.activation(k_all[:, :, m, 0:NTEXT], bank[m][:, 0:TT].rearrange("p (b k) -> p b k", b=B),
                                             ACT.Copy, scale=SCALE).then_inc(k_text_act, 1)
                    for c in range(KI0 + RING, VI0 + RING):
                        round_chunk(c)
                    act.wait_ge(k_ip_ready, 1)
                    nc.scalar.activation(k_ip[:, 0:HALF], bank[5][:, 0:HALF], ACT.Copy).then_inc(k_ip_act, 1)
                    for c in range(VI0 + RING, len(chunks)):
                        round_chunk(c)
                    act.wait_ge(v_ip_ready, 1)
                    nc.scalar.activation(v_ip[:, 0:HALF], bank[7][:, 0:HALF], ACT.Copy).then_inc(v_ip_act, 1)
                    for n, (m0, m1) in enumerate(((0, KD - 1), (KD - 1, KD))):
                        act.wait_ge(k_ipT_ready, n + 1)
                        nc.scalar.activation(
                            k_all[:, :, m0:m1, NTEXT:KEYS].rearrange("p b m k -> p m b k"),
                            bank[1 + n][:, 0:(m1 - m0) * P].rearrange("p (m n) -> p m n", n=P)[:, :, P - TI:P].rearrange("p m (b k) -> p m b k", b=B),
                            ACT.Copy, scale=SCALE).then_inc(k_ipT_act, 1)

                @block.vector
                def _(dve):
                    for k in range(KC):
                        dve.wait_ge(ctxT_hi_done, k + 1)
                        nc.vector.tensor_tensor(ctxT_lo[:, k, :], bank[k][:], ctxT_hi[:, k, :].bitcast(F32), ALU.subtract).then_inc(ctxT_lo_done, 1)

                    steps = [0]

                    def step(ins):
                        ins.then_inc(mask_step, 1)
                        steps[0] += 1
                        dve.wait_ge(mask_step, steps[0])

                    def edge(f, cols=None):
                        e = boxes[:, :, f]
                        return e if cols is None else e.unsqueeze(2).broadcast_to([P, B * BOXES, cols])

                    dve.wait_ge(small_loaded, 64)
                    y_all = gy[:].unsqueeze(1).broadcast_to([P, B * BOXES, TPB])
                    nc.vector.tensor_scalar(in_x[:, 0, :], edge(0), gx[:, 0:1], None, ALU.is_le)
                    nc.vector.tensor_scalar(in_x[:, 1, :], edge(2), gx[:, 0:1], None, ALU.is_ge)
                    nc.vector.tensor_tensor(in_y[:, 0, :, :], y_all, edge(1, TPB), ALU.is_ge)
                    step(nc.vector.tensor_tensor(in_y[:, 1, :, :], y_all, edge(3, TPB), ALU.is_le))
                    step(nc.vector.tensor_tensor(in_x[:, 0, :], in_x[:, 0, :], in_x[:, 1, :], ALU.mult))
                    step(nc.vector.tensor_tensor(in_y[:, 0, :, :], in_y[:, 0, :, :], in_y[:, 1, :, :], ALU.mult))
                    ins_all = inside[:].rearrange("p b m t -> p (b m) t")
                    step(nc.vector.tensor_tensor(ins_all, in_y[:, 0, :, :], in_x[:, 0, :].unsqueeze(2).broadcast_to([P, B * BOXES, TPB]), ALU.mult))
                    step(nc.vector.tensor_reduce(any_in[:], inside[:].rearrange("p b m t -> p b t m"), AX.X, ALU.max))
                    mask_b = mask[:].rearrange("p (b t) k -> p b t k", b=B)
                    for n in range(BOXES):
                        nc.vector.tensor_scalar(mask_b[:, :, :, n], any_in[:], NEG, None, ALU.mult)
                        last = nc.vector.tensor_scalar(mask_b[:, :, :, BOXES + n], inside[:, :, n, :], 1.0, -NEG, ALU.subtract, ALU.mult)
                    step(last)

                    for i in range(NPB):
                        dve.wait_ge(v_text_ready, 2 * i + 2)
                        nc.vector.tensor_copy(v_text[:, i, HALF:D], bank[2 * i + 1][0:PB, 0:HALF]).then_inc(v_text_dve, 1)
                    for m in range(1, KD, 2):
                        dve.wait_ge(k_text_ready, m + 1)
                        nc.vector.tensor_scalar(k_all[:, :, m, 0:NTEXT], bank[m][:, 0:TT].rearrange("p (b k) -> p b k", b=B),
                                                SCALE, None, ALU.mult).then_inc(k_text_dve, 1)
                    dve.wait_ge(k_ip_ready, 2)
                    nc.vector.tensor_copy(k_ip[:, HALF:D], bank[6][:, 0:HALF]).then_inc(k_ip_dve, 1)
                    dve.wait_ge(v_ip_ready, 2)
                    nc.vector.tensor_copy(v_ip[:, HALF:D], bank[0][:, 0:HALF]).then_inc(v_ip_dve, 1)

                @block.tensor
                def _(pe):
                    pe.wait_ge(ident_made, 1)
                    pe.wait_ge(ctx_loaded, 16 * (2 + B))
                    for k in range(KC):
                        cols = slice(k * P, (k + 1) * P)
                        for i in range(NPB):
                            nc.tensor.transpose(bank[k][:, i * PB:(i + 1) * PB], ctx_text[:, i, cols], ident[0:PB, 0:PB])
                        nc.tensor.transpose(bank[k][:, TT:TT + TI], ctx_ip[:, cols], ident[0:TI, 0:TI]).then_inc(ctxT_ready, 1)

                    def three(dst, a_hi, a_lo, b_hi, b_lo, first, last):
                        nc.tensor.matmul(dst, a_hi, b_hi, start=first, stop=False)
                        nc.tensor.matmul(dst, a_hi, b_lo, start=False, stop=False)
                        return nc.tensor.matmul(dst, a_lo, b_hi, start=False, stop=last)

                    def tokens_times_w(c, toks, h, dst, first, last):
                        k, s, cols = c % KC, c % RING, slice(h * HALF, (h + 1) * HALF)
                        return three(dst, ctxT_hi[:, k, toks], ctxT_lo[:, k, toks], w_hi[:, s, cols], w_lo[:, s, cols], first, last)

                    pe.wait_ge(ctxT_lo_done, KC)
                    for k in range(KC):
                        pe.wait_ge(w_lo_done, V0 + k + 1)
                        for n in range(2 * NPB):
                            i, h = n // 2, n % 2
                            ins = tokens_times_w(V0 + k, slice(i * PB, (i + 1) * PB), h, bank[n][0:PB, 0:HALF], k == 0, k == KC - 1)
                            if k == KC - 1:
                                ins.then_inc(v_text_ready, 1)
                        if k < KC - 1:
                            ins.then_inc(w_used, 1)
                    for k in range(KC):
                        pe.wait_ge(w_lo_done, K0 + k + 1)
                        s = (K0 + k) % RING
                        for m in range(KD):
                            if k == 0:
                                pe.wait_ge(v_text_dve if m % 2 else v_text_act, m // 2 + 1)
                            rows = slice(m * P, (m + 1) * P)
                            ins = three(bank[m][:, 0:TT], w_hi[:, s, rows], w_lo[:, s, rows], ctxT_hi[:, k, 0:TT], ctxT_lo[:, k, 0:TT],
                                        k == 0, k == KC - 1)
                            if k == KC - 1:
                                ins.then_inc(k_text_ready, 1)
                        if k < KC - 1:
                            ins.then_inc(w_used, 1)
                    ip_toks = slice(TT + TI - P, TT + TI)
                    for k in range(KC):
                        pe.wait_ge(w_lo_done, KI0 + k + 1)
                        for h in range(2):
                            if k == 0:
                                pe.wait_ge(v_text_act if h else v_text_dve, NPB if h else NPB - 1)
                            ins = tokens_times_w(KI0 + k, ip_toks, h, bank[5 + h][:, 0:HALF], k == 0, k == KC - 1)
                            if k == KC - 1:
                                ins.then_inc(k_ip_ready, 1)
                        if k < KC - 1:
                            ins.then_inc(w_used, 1)
                    for k in range(KC):
                        pe.wait_ge(w_lo_done, VI0 + k + 1)
                        for h in range(2):
                            if k == 0:
                                pe.wait_ge(k_text_act if h else v_text_dve, 1 if h else NPB)
                            ins = tokens_times_w(VI0 + k, ip_toks, h, bank[0 if h else 7][:, 0:HALF], k == 0, k == KC - 1)
                            if k == KC - 1:
                                ins.then_inc(v_ip_ready, 1)
                        if k < KC - 1:
                            ins.then_inc(w_used, 1)
                    pe.wait_ge(k_ip_act, 1)
                    pe.wait_ge(k_ip_dve, 1)
                    pe.wait_ge(k_text_dve, 1)
                    pe.wait_ge(k_text_act, 2)
                    for m in range(KD):
                        ins = nc.tensor.transpose(bank[1 + m // (KD - 1)][:, m % (KD - 1) * P:(m % (KD - 1) + 1) * P], k_ip[:, m * P:(m + 1) * P], ident[:])
                        if m >= KD - 2:
                            ins.then_inc(k_ipT_ready, 1)

        res = sb("res", [P, 2, GT, D])
        xT_hi, xT_lo = sb("xT_hi", [P, KD, GQ], F32R), sb("xT_lo", [P, KD, GQ], F32R)
        pT_hi, pT_lo, PT_RING = xT_hi, xT_lo, KD
        qT_hi, qT_lo = sb("qT_hi", [P, KD, GQ], F32R), sb("qT_lo", [P, KD, GQ], F32R)
        prob = sb("prob", [P, GT * SW])
        oT_hi, oT_lo = sb("oT_hi", [P, KD, GQ], F32R), sb("oT_lo", [P, KD, GQ], F32R)
        zero = sb("zero", [P, 1])
        k_raw, v_raw = sb("k_raw", [P, KD, KEYS]), sb("v_raw", [P, D])
        k_hi, k_lo = sb("k_hi", [P, KD, HPT, KEYS], F32R), sb("k_lo", [P, KD, HPT, KEYS], F32R)
        v_hi, v_lo = sb("v_hi", [P, PAIRS * P], F32R), sb("v_lo", [P, PAIRS * P], F32R)
        top, total, inv = sb("top", [P, GT, 2, HEADS]), sb("total", [P, GT, 2, HEADS]), sb("inv", [P, GT, 2, HEADS])

        s_bank, t_bank, p_bank, o_bank = bank[0:2], bank[2:4], bank[4:6], bank[6:8]

        k_raw_loaded, v_raw_loaded = sem("k_raw_loaded"), sem("v_raw_loaded")
        kv_zeroed, k_built, v_built, k_hi_built, v_hi_built = (sem(n) for n in ("kv_zeroed", "k_built", "v_built", "k_hi_built", "v_hi_built"))
        score_ready, xT_ready, q_ready, pT_ready, pv_ready, out_ready = (
            sem(n) for n in ("score_ready", "xT_ready", "q_ready", "pT_ready", "pv_ready", "out_ready"))
        score_copied, xT_hi_done, q_hi_done, pT_hi_done, pv_hi_done, exp_done = (
            sem(n) for n in ("score_copied", "xT_hi_done", "q_hi_done", "pT_hi_done", "pv_hi_done", "exp_done"))
        xT_lo_done, q_lo_done, pT_lo_done, pv_lo_done, max_done, sum_done, inv_done, out_done = (
            sem(n) for n in ("xT_lo_done", "q_lo_done", "pT_lo_done", "pv_lo_done", "max_done", "sum_done", "inv_done", "out_done"))
        mask_added, max_subbed, prob_done, res_done = (sem(n) for n in ("mask_added", "max_subbed", "prob_done", "res_done"))
        stored = [sem("stored0"), sem("stored1")]

        def wait(eng, s, value):
            if not (isinstance(value, int) and value <= 0):
                eng.wait_ge(s, value)

        def units_for_tile(t):
            return -(-(t + 1) * SW // 512)

        def tile(t):
            return prob[:, t * SW:(t + 1) * SW].rearrange("p (h k) -> p h k", k=KEYS)

        SPANS = ((0, NTEXT), (NTEXT, KEYS))

        with nc.Block() as block:

            @block.sync
            def _(sp):
                def load_k(b):
                    wait(sp, k_built, HPT * b)
                    sp.dma_start(k_raw[:].rearrange("p m k -> p (m k)"), k_scratch[:, b, :]).then_inc(k_raw_loaded, 16)

                def load_v(b):
                    wait(sp, v_built, 4 * b)
                    for h in range(2):
                        sp.dma_start(v_raw[h * KEYS:(h + 1) * KEYS, :], v_scratch[b]).then_inc(v_raw_loaded, 16)

                def load_x(g, u):
                    sp.wait_ge(xT_ready, KD * (g + 1))
                    sp.wait_ge(res_done, g + 1)
                    sp.dma_start(xin[:, u, :, :], x_g[g + 2]).then_inc(x_loaded[u], 16)

                def store(g, u, t):
                    sp.wait_ge(out_done, 2 * GT * g + 2 * (t + 1))
                    sp.dma_start(out_t[g, t], res[:, u, t, :]).then_inc(stored[u], 16)

                def group(g, u, b, stores, loads_x, loads_kv):
                    if loads_kv and u == 0:
                        load_k(b + 1)
                    if loads_kv and u == 1:
                        load_v(b + 1)
                    if stores:
                        store(g - 1, 1 - u, 0)
                        store(g - 1, 1 - u, 1)
                    if loads_x:
                        load_x(g, u)
                    if stores:
                        store(g - 1, 1 - u, 2)
                        store(g - 1, 1 - u, 3)

                load_k(0)
                load_v(0)
                group(0, 0, 0, False, True, True)
                with sp.Fori(0, B - 2) as i:
                    group(2 * i + 1, 1, i, True, True, True)
                    group(2 * i + 2, 0, i + 1, True, True, True)
                group(NG - 3, 1, B - 2, True, True, True)
                group(NG - 2, 0, B - 1, True, False, False)
                group(NG - 1, 1, B - 1, True, False, False)
                for t in range(GT):
                    store(NG - 1, 1, t)
                for u in range(2):
                    sp.wait_ge(stored[u], 16 * GT * NG // 2)

            @block.gpsimd
            def _(pool):
                def build_k(b):
                    pool.wait_ge(k_raw_loaded, 16 * (b + 1))
                    wait(pool, score_ready, UNITS * GPB * b)
                    for j in range(HPT):
                        rows = slice(j * DH, (j + 1) * DH)
                        nc.gpsimd.tensor_tensor(k_hi[rows, :, j, :], k_raw[rows, :, :], zero[rows, :].unsqueeze(2).broadcast_to([DH, KD, KEYS]), ALU.add).then_inc(k_hi_built, 1)
                    pool.wait_ge(k_hi_built, HPT * (b + 1))
                    for j in range(HPT):
                        rows = slice(j * DH, (j + 1) * DH)
                        nc.gpsimd.tensor_tensor(k_lo[rows, :, j, :], k_raw[rows, :, :], k_hi[rows, :, j, :].bitcast(F32), ALU.subtract).then_inc(k_built, 1)
                    pool.wait_ge(k_built, HPT * (b + 1))

                def v_cols(v, j):
                    half = v[j * KEYS:(j + 1) * KEYS, :].rearrange("p (m c) -> p m c", c=2 * P)
                    return [half[:, :, i * (P + P // 2) + j * DH:i * (P + P // 2) + (j + 1) * DH] for i in range(2)]

                def v_src(j):
                    half = v_raw[j * KEYS:(j + 1) * KEYS, :].rearrange("p (m c) -> p m c", c=P)
                    return [half[:, :, i * P // 2 + j * DH:i * P // 2 + (j + 1) * DH] for i in range(2)]

                def build_v(b, g):
                    pool.wait_ge(v_raw_loaded, 32 * (b + 1))
                    wait(pool, pv_ready, KD * g)
                    for j in range(2):
                        for dst, src in zip(v_cols(v_hi, j), v_src(j)):
                            nc.gpsimd.tensor_tensor(dst, src, zero[j * KEYS:(j + 1) * KEYS, :].unsqueeze(2).broadcast_to([KEYS, KD, DH]), ALU.add).then_inc(v_hi_built, 1)
                    pool.wait_ge(v_hi_built, 4 * (b + 1))
                    for j in range(2):
                        for dst, src, hi in zip(v_cols(v_lo, j), v_src(j), v_cols(v_hi, j)):
                            nc.gpsimd.tensor_tensor(dst, src, hi.bitcast(F32), ALU.subtract).then_inc(v_built, 1)
                    pool.wait_ge(v_built, 4 * (b + 1))

                def add_mask(g, t):
                    pool.wait_ge(score_copied, UNITS * g + units_for_tile(t))
                    ip = tile(t)[:, :, NTEXT:KEYS]
                    m = mask[:, GT * g + t, :].unsqueeze(1).broadcast_to([P, HEADS, NIP])
                    nc.gpsimd.tensor_tensor(ip, ip, m, ALU.add).then_inc(mask_added, 1)

                def sub_max(g, t):
                    pool.wait_ge(max_done, GT * g + t + 1)
                    for n, (k0, k1) in enumerate(SPANS):
                        s = tile(t)[:, :, k0:k1]
                        m = top[:, t, n, :].unsqueeze(2).broadcast_to([P, HEADS, k1 - k0])
                        ins = nc.gpsimd.tensor_tensor(s, s, m, ALU.subtract)
                    ins.then_inc(max_subbed, 1)

                def normalise(g, t):
                    pool.wait_ge(inv_done, GT * g + t + 1)
                    for n, (k0, k1) in enumerate(SPANS):
                        s = tile(t)[:, :, k0:k1]
                        r = inv[:, t, n, :].unsqueeze(2).broadcast_to([P, HEADS, k1 - k0])
                        ins = nc.gpsimd.tensor_tensor(s, s, r, ALU.mult)
                    ins.then_inc(prob_done, 1)

                def residual(g, u, n):
                    pool.wait_ge(x_loaded[u], 16 * (n + 1))
                    wait(pool, stored[u], 16 * GT * n)
                    nc.gpsimd.tensor_tensor(res[:, u, :, :], xin[:, u, :, :], bias[:].unsqueeze(1).broadcast_to([P, GT, D]), ALU.add).then_inc(res_done, 1)

                def group(g, u, b, builds_v, builds_k):
                    add_mask(g, 0)
                    add_mask(g, 1)
                    sub_max(g, 0)
                    add_mask(g, 2)
                    sub_max(g, 1)
                    add_mask(g, 3)
                    sub_max(g, 2)
                    sub_max(g, 3)
                    if builds_v:
                        pool.wait_ge(max_subbed, GT * (g + 1))
                        build_v(b, g)
                    residual(g, u, b)
                    for t in range(GT):
                        normalise(g, t)
                    if builds_k:
                        pool.wait_ge(prob_done, GT * (g + 1))
                        build_k(b + 1)

                for buf in (k_hi[:].rearrange("p m j k -> p (m j k)"), k_lo[:].rearrange("p m j k -> p (m j k)"), v_hi[:], v_lo[:], zero[:]):
                    nc.gpsimd.memset(buf if buf.dtype == F32 else buf.bitcast(F32), 0.0).then_inc(kv_zeroed, 1)
                pool.wait_ge(kv_zeroed, 5)
                build_k(0)
                build_v(0, 0)
                group(0, 0, 0, False, False)
                with pool.Fori(0, B - 1) as i:
                    group(2 * i + 1, 1, i, False, True)
                    group(2 * i + 2, 0, i + 1, True, False)
                group(NG - 1, 1, B - 1, False, False)

            @block.scalar
            def _(act):
                def hi_part(ready, count, dst, src, done):
                    act.wait_ge(ready, count)
                    nc.scalar.activation(dst, src[:], ACT.Copy).then_inc(done, 1)

                def copy_scores(g, u):
                    act.wait_ge(score_ready, UNITS * g + u + 1)
                    nc.scalar.activation(prob[:, u * 512:(u + 1) * 512], s_bank[u % 2][:], ACT.Copy).then_inc(score_copied, 1)

                def exponentials(g, t):
                    act.wait_ge(max_subbed, GT * g + t + 1)
                    nc.scalar.activation(prob[:, t * SW:(t + 1) * SW], prob[:, t * SW:(t + 1) * SW], ACT.Exp).then_inc(exp_done, 1)

                def xT_part(g, k):
                    hi_part(xT_ready, KD * g + k + 1, xT_hi[:, k, :], t_bank[k % 2], xT_hi_done)

                def q_part(g, m):
                    hi_part(q_ready, KD * g + m + 1, qT_hi[:, m, :], p_bank[m % 2], q_hi_done)

                def pT_part(g, p):
                    hi_part(pT_ready, PAIRS * g + p + 1, pT_hi[:, p % PT_RING, :], t_bank[(p + 1) % 2], pT_hi_done)

                def pv_part(g, m):
                    hi_part(pv_ready, KD * g + m + 1, oT_hi[:, m, :], p_bank[(m + 1) % 2], pv_hi_done)

                def group(g, more):
                    for u in range(UNITS):
                        copy_scores(g, u)
                    exponentials(g, 0)
                    for k in range(KD):
                        if more:
                            xT_part(g + 1, k)
                        if k + 1 < GT:
                            exponentials(g, k + 1)
                    if more:
                        for m in range(KD):
                            q_part(g + 1, m)
                    for p in range(4):
                        pT_part(g, p)
                    for m in range(3):
                        pv_part(g, m)
                        pT_part(g, 2 * m + 4)
                        pT_part(g, 2 * m + 5)
                    pv_part(g, 3)
                    pv_part(g, 4)

                for k in range(KD):
                    xT_part(0, k)
                for m in range(KD):
                    q_part(0, m)
                group(0, True)
                with act.Fori(0, B - 1) as i:
                    group(2 * i + 1, True)
                    group(2 * i + 2, True)
                group(NG - 1, False)

            @block.vector
            def _(dve):
                def lo_part(hi_done, count, dst, src, hi, done):
                    dve.wait_ge(hi_done, count)
                    nc.vector.tensor_tensor(dst, src[:], hi.bitcast(F32), ALU.subtract).then_inc(done, 1)

                def xT_part(g, k):
                    lo_part(xT_hi_done, KD * g + k + 1, xT_lo[:, k, :], t_bank[k % 2], xT_hi[:, k, :], xT_lo_done)

                def q_part(g, m):
                    lo_part(q_hi_done, KD * g + m + 1, qT_lo[:, m, :], p_bank[m % 2], qT_hi[:, m, :], q_lo_done)

                def pT_part(g, p):
                    s = p % PT_RING
                    lo_part(pT_hi_done, PAIRS * g + p + 1, pT_lo[:, s, :], t_bank[(p + 1) % 2], pT_hi[:, s, :], pT_lo_done)

                def pv_part(g, m):
                    lo_part(pv_hi_done, KD * g + m + 1, oT_lo[:, m, :], p_bank[(m + 1) % 2], oT_hi[:, m, :], pv_lo_done)

                def maxima(g, t):
                    dve.wait_ge(mask_added, GT * g + t + 1)
                    for n, (k0, k1) in enumerate(SPANS):
                        ins = nc.vector.tensor_reduce(top[:, t, n, :], tile(t)[:, :, k0:k1], AX.X, ALU.max)
                    ins.then_inc(max_done, 1)

                def sums(g, t):
                    dve.wait_ge(exp_done, GT * g + t + 1)
                    for n, (k0, k1) in enumerate(SPANS):
                        ins = nc.vector.tensor_reduce(total[:, t, n, :], tile(t)[:, :, k0:k1], AX.X, ALU.add)
                        ins.then_inc(sum_done, 1)
                    dve.wait_ge(sum_done, 2 * (GT * g + t + 1))
                    nc.vector.reciprocal(inv[:, t, :, :], total[:, t, :, :]).then_inc(inv_done, 1)

                def output(g, u, j):
                    t, h = j // 2, j % 2
                    r = res[:, u, t, h * HALF:(h + 1) * HALF]
                    if j == 0:
                        dve.wait_ge(res_done, g + 1)
                    dve.wait_ge(out_ready, 2 * GT * g + j + 1)
                    nc.vector.tensor_tensor(r, o_bank[h][:, 0:HALF], r, ALU.add).then_inc(out_done, 1)

                def group(g, u, before, more):
                    for t in range(GT):
                        maxima(g, t)
                    for k in range(KD):
                        if before:
                            output(g - 1, 1 - u, k)
                        if more:
                            xT_part(g + 1, k)
                        if k in (1, 2):
                            sums(g, k - 1)
                    for m in range(KD):
                        if more:
                            q_part(g + 1, m)
                        if m in (0, 1):
                            sums(g, m + 2)
                    pT_part(g, 0)
                    pT_part(g, 1)
                    if before:
                        output(g - 1, 1 - u, 5)
                    pT_part(g, 2)
                    pT_part(g, 3)
                    if before:
                        output(g - 1, 1 - u, 6)
                        output(g - 1, 1 - u, 7)
                    for m in range(3):
                        pv_part(g, m)
                        pT_part(g, 2 * m + 4)
                        pT_part(g, 2 * m + 5)
                    pv_part(g, 3)
                    pv_part(g, 4)

                for k in range(KD):
                    xT_part(0, k)
                for m in range(KD):
                    q_part(0, m)
                group(0, 0, False, True)
                with dve.Fori(0, B - 1) as i:
                    group(2 * i + 1, 1, True, True)
                    group(2 * i + 2, 0, True, True)
                group(NG - 1, 1, True, False)
                for j in range(2 * GT):
                    output(NG - 1, 1, j)

            @block.tensor
            def _(pe):
                def three(dst, a_hi, a_lo, b_hi, b_lo, first, last):
                    nc.tensor.matmul(dst, a_hi, b_hi, start=first, stop=False)
                    nc.tensor.matmul(dst, a_hi, b_lo, start=False, stop=False)
                    return nc.tensor.matmul(dst, a_lo, b_hi, start=False, stop=last)

                def score_unit(g, u, b, new_batch):
                    wait(pe, score_copied, UNITS * g + u - 1)
                    if u == 0 and new_batch:
                        pe.wait_ge(k_built, HPT * (b + 1))
                    for half in range(2):
                        t, m = divmod(2 * u + half, KD)
                        if t == 0:
                            pe.wait_ge(q_lo_done, KD * g + m + 1)
                        q_cols = slice(t * P, (t + 1) * P)
                        flat = [k[:, m, :, :].rearrange("p j k -> p (j k)") for k in (k_hi, k_lo)]
                        ins = three(s_bank[u % 2][:, half * CW:(half + 1) * CW], qT_hi[:, m, q_cols], qT_lo[:, m, q_cols], *flat, True, True)
                    ins.then_inc(score_ready, 1)

                def x_transpose(g, u, n, k):
                    if k == 0:
                        pe.wait_ge(x_loaded[u], 16 * (n + 1))
                    if k < 2:
                        wait(pe, pT_lo_done, PAIRS * (g - 1))
                    else:
                        pe.wait_ge(xT_lo_done, KD * g + k - 1)
                    for t in range(GT):
                        ins = nc.tensor.transpose(t_bank[k % 2][:, t * P:(t + 1) * P], xin[:, u, t, k * P:(k + 1) * P], ident[:])
                    ins.then_inc(xT_ready, 1)

                def q_tile(g, m):
                    if m < 2:
                        wait(pe, pv_lo_done, KD * (g - 1))
                    else:
                        pe.wait_ge(q_lo_done, KD * g + m - 1)
                    cols = slice(m * P, (m + 1) * P)
                    for k in range(KD):
                        if m == 0:
                            pe.wait_ge(xT_lo_done, KD * g + k + 1)
                        ins = three(p_bank[m % 2][:], wq_hi[:, k, cols], wq_lo[:, k, cols], xT_hi[:, k, :], xT_lo[:, k, :], k == 0, k == KD - 1)
                    ins.then_inc(q_ready, 1)

                def p_transpose(g, p, more):
                    if p < 2:
                        wait(pe, xT_lo_done, KD * (g + 2) if more else KD * (g + 1))
                        if not more:
                            pe.wait_ge(pT_lo_done, PAIRS * g)
                    else:
                        pe.wait_ge(pT_lo_done, PAIRS * g + p - 1)
                    for t in range(GT):
                        if p == 0:
                            pe.wait_ge(prob_done, GT * g + t + 1)
                        src = prob[:, t * SW + p * P:t * SW + (p + 1) * P]
                        ins = nc.tensor.transpose(t_bank[(p + 1) % 2][:, t * P:(t + 1) * P], src, ident[:])
                    ins.then_inc(pT_ready, 1)

                def pv_tile(g, m, b, new_batch, more):
                    if m == 0 and new_batch:
                        pe.wait_ge(v_built, 4 * (b + 1))
                    if m < 2:
                        pe.wait_ge(q_lo_done, KD * (g + 2) if more else KD * (g + 1))
                        if not more:
                            pe.wait_ge(pv_lo_done, KD * g)
                    else:
                        pe.wait_ge(pv_lo_done, KD * g + m - 1)
                    pe.wait_ge(pT_lo_done, PAIRS * g + 2 * m + 2)
                    for i in range(2):
                        p = 2 * m + i
                        s, cols = p % PT_RING, slice(p * P, (p + 1) * P)
                        ins = three(p_bank[(m + 1) % 2][:], v_hi[:, cols], v_lo[:, cols], pT_hi[:, s, :], pT_lo[:, s, :], i == 0, i == 1)
                    ins.then_inc(pv_ready, 1)

                def out_half(g, j):
                    t, h = j // 2, j % 2
                    if j == 0:
                        pe.wait_ge(pv_lo_done, KD * (g + 1))
                    if j >= 2:
                        pe.wait_ge(out_done, 2 * GT * g + j - 1)
                    rows, cols = slice(t * P, (t + 1) * P), slice(h * HALF, (h + 1) * HALF)
                    for k in range(KD):
                        ins = three(o_bank[h][:, 0:HALF], oT_hi[:, k, rows], oT_lo[:, k, rows], wo_hi[:, k, cols], wo_lo[:, k, cols], k == 0, k == KD - 1)
                    ins.then_inc(out_ready, 1)

                def group(g, u, b, new_batch, n_next, before, more):
                    for n in range(UNITS):
                        score_unit(g, n, b, new_batch)
                    for k in range(KD):
                        if before:
                            out_half(g - 1, k)
                        if more:
                            x_transpose(g + 1, 1 - u, n_next, k)
                    if more:
                        for m in range(KD):
                            q_tile(g + 1, m)
                    p_transpose(g, 0, more)
                    p_transpose(g, 1, more)
                    if before:
                        out_half(g - 1, 5)
                    p_transpose(g, 2, more)
                    p_transpose(g, 3, more)
                    if before:
                        out_half(g - 1, 6)
                        out_half(g - 1, 7)
                    for m in range(3):
                        pv_tile(g, m, b, new_batch, more)
                        p_transpose(g, 2 * m + 4, more)
                        p_transpose(g, 2 * m + 5, more)
                    pv_tile(g, 3, b, new_batch, more)
                    pv_tile(g, 4, b, new_batch, more)

                for k in range(KD):
                    x_transpose(0, 0, 0, k)
                for m in range(KD):
                    q_tile(0, m)
                group(0, 0, 0, True, 0, False, True)
                with pe.Fori(0, B - 1) as i:
                    group(2 * i + 1, 1, i, False, i + 1, True, True)
                    group(2 * i + 2, 0, i + 1, True, i + 1, True, True)
                group(NG - 1, 1, B - 1, False, B, True, False)
                for j in range(2 * GT):
                    out_half(NG - 1, j)


_INS = ["x", "ctx_2048", "fside_Bx4x4_0", "L0_xattn_w_q", "L0_xattn_w_k", "L0_xattn_w_v", "L0_xattn_w_k_ip",
        "L0_xattn_w_v_ip", "L0_xattn_w_out", "L0_xattn_b_out"]


def kernel(**inputs):
    import numpy as np
    import concourse.bacc as bacc
    from concourse.bass_utils import run_bass_kernel_spmd

    nc = bacc.Bacc("TRN2", target_bir_lowering=False, num_devices=1)
    arrays, args = {}, []
    for name in _INS:
        a = np.ascontiguousarray(inputs[name])
        arrays[f"in_{name}"] = a
        args.append(nc.dram_tensor(f"in_{name}", a.shape, mybir.dt.from_np(a.dtype), kind="ExternalInput").ap())
    seq = inputs["x"].shape[1]
    line = np.arange(GRID, dtype=np.float32) * np.float32(1.0 / (GRID - 1))
    n = np.arange(seq).reshape(seq // P, P).T
    for name, g in (("grid_x", line[n[:, 0:1] % GRID]), ("grid_y", line[n // GRID])):
        g = np.ascontiguousarray(g)
        arrays[name] = g
        args.append(nc.dram_tensor(name, g.shape, F32, kind="ExternalInput").ap())
    shape = tuple(inputs["x"].shape)
    args.append(nc.dram_tensor("out", shape, F32, kind="ExternalOutput").ap())
    attention_kernel(nc, *args)
    r = run_bass_kernel_spmd(nc, [arrays], core_ids=[0])
    return r.results[0]["out"]
```

```python
from contextlib import ExitStack

import concourse.bass as bass
from concourse import mybir

F32 = mybir.dt.float32
F32R = mybir.dt.float32r
ACT = mybir.ActivationFunctionType
ALU = mybir.AluOpType
AX = mybir.AxisListType

P = 128
HEADS, DH = 20, 32
NIP = 8
BOXES = 4
NEG = -10000.0
GRID = 32
GQ = 512
GT = GQ // P
RING = 4


def attention_kernel(nc, xT_dram, textT, ipT, bbox, w_q, w_k, w_v, w_k_ip, w_v_ip, w_out, b_out, grid_x, grid_y, outT):
    B, D, S = xT_dram.shape
    C, TT = textT.shape
    TI = ipT.shape[1]
    NTEXT = TT // B
    KEYS = NTEXT + NIP
    KD, KC = D // P, C // P
    GPB = S // GQ
    NG = B * GPB
    TPB = S // P
    HPT = P // DH
    PAIRS = HEADS // 2
    HP = P // 2
    CW = HPT * KEYS
    SW = HEADS * KEYS
    UNITS = GT * SW // 512
    HALF = D // 2
    PB = 2 * NTEXT
    NPB = B // 2
    SCALE = float(DH) ** -0.5

    x_half = xT_dram.rearrange("b (k p) (h q) -> h b p k q", p=P, q=GQ)
    out_half = outT.rearrange("b (m p) (h q) -> h b m p q", p=P, q=GQ)
    k_scratch = nc.dram_tensor("k_scratch", (P, B, KD * KEYS), F32).ap()
    v_scratch = nc.dram_tensor("v_scratch", (B, KEYS, D), F32).ap()

    whole = ExitStack()
    with whole:
        def sb(name, shape, dt=F32, stack=whole):
            return stack.enter_context(nc.sbuf_tensor(name, shape, dt))

        def sem(name):
            return whole.enter_context(nc.semaphore(name))

        bank = [whole.enter_context(nc.psum_tensor(f"bank{i}", [P, 512], F32)) for i in range(8)]

        ident = sb("ident", [P, P])
        wq_hi, wq_lo = sb("wq_hi", [P, KD, D], F32R), sb("wq_lo", [P, KD, D], F32R)
        wo_hi, wo_lo = sb("wo_hi", [P, KD, D], F32R), sb("wo_lo", [P, KD, D], F32R)
        xin = sb("xin", [P, 2, KD, GQ])
        xT_hi, xT_lo = sb("xT_hi", [P, KD * GQ], F32R), sb("xT_lo", [P, KD * GQ], F32R)
        qT_hi, qT_lo = sb("qT_hi", [P, KD, GQ], F32R), sb("qT_lo", [P, KD, GQ], F32R)
        k_hi, k_lo = sb("k_hi", [P, KD, HPT, KEYS], F32R), sb("k_lo", [P, KD, HPT, KEYS], F32R)
        k_raw = sb("k_raw", [P, KD, KEYS])
        mask = sb("mask", [P, B * TPB, NIP])
        bias = sb("bias", [P, KD])

        x_loaded = [sem("x_loaded0"), sem("x_loaded1")]
        small_loaded, ident_zeroed, ident_made = sem("small_loaded"), sem("ident_zeroed"), sem("ident_made")
        xT_hi_done, xT_lo_done = sem("xT_hi_done"), sem("xT_lo_done")
        q_ready, q_hi_done, q_lo_done = sem("q_ready"), sem("q_hi_done"), sem("q_lo_done")
        k_zeroed, k_raw_loaded, k_hi_built, k_built = (sem(n) for n in ("k_zeroed", "k_raw_loaded", "k_hi_built", "k_built"))

        l_bank = bank[6:8]

        def wait(eng, s, value):
            if not (isinstance(value, int) and value <= 0):
                eng.wait_ge(s, value)

        def three(dst, a_hi, a_lo, b_hi, b_lo, first, last):
            nc.tensor.matmul(dst, a_hi, b_hi, start=first, stop=False)
            nc.tensor.matmul(dst, a_hi, b_lo, start=False, stop=False)
            return nc.tensor.matmul(dst, a_lo, b_hi, start=False, stop=last)


        def x_tile(t, k):
            return t[:, k * GQ:(k + 1) * GQ]

        def x_hi_part(act, g, u, k):
            nc.scalar.activation(x_tile(xT_hi, k), xin[:, u, k, :], ACT.Copy).then_inc(xT_hi_done, 1)

        def x_lo_part(dve, g, u, k):
            dve.wait_ge(xT_hi_done, KD * g + k + 1)
            nc.vector.tensor_tensor(x_tile(xT_lo, k), xin[:, u, k, :], x_tile(xT_hi, k).bitcast(F32), ALU.subtract).then_inc(xT_lo_done, 1)

        def q_steps(pe, g, m, k0=0, k1=KD):
            cols = slice(m * P, (m + 1) * P)
            for k in range(k0, k1):
                if m == 0:
                    pe.wait_ge(xT_lo_done, KD * g + k + 1)
                ins = three(l_bank[(m + 1) % 2][:], wq_hi[:, k, cols], wq_lo[:, k, cols], x_tile(xT_hi, k), x_tile(xT_lo, k), k == 0, k == KD - 1)
            if k1 == KD:
                ins.then_inc(q_ready, 1)

        def q_hi_part(act, g, m):
            act.wait_ge(q_ready, KD * g + m + 1)
            nc.scalar.activation(qT_hi[:, m, :], l_bank[(m + 1) % 2][:], ACT.Copy).then_inc(q_hi_done, 1)

        def q_lo_part(dve, g, m):
            dve.wait_ge(q_hi_done, KD * g + m + 1)
            nc.vector.tensor_tensor(qT_lo[:, m, :], l_bank[(m + 1) % 2][:], qT_hi[:, m, :].bitcast(F32), ALU.subtract).then_inc(q_lo_done, 1)

        def k_head(t, j):
            return t[j * DH:(j + 1) * DH, :, j, :]

        def k_hi_part(act, b):
            act.wait_ge(k_raw_loaded, 16 * (b + 1))
            for j in range(HPT):
                nc.scalar.activation(k_head(k_hi, j), k_raw[j * DH:(j + 1) * DH, :, :], ACT.Copy).then_inc(k_hi_built, 1)

        def k_lo_part(dve, b):
            for j in range(HPT):
                dve.wait_ge(k_hi_built, HPT * b + j + 1)
                nc.vector.tensor_tensor(k_head(k_lo, j), k_raw[j * DH:(j + 1) * DH, :, :], k_head(k_hi, j).bitcast(F32), ALU.subtract).then_inc(k_built, 1)

        def load_k(sp, b):
            sp.dma_start(k_raw[:].rearrange("p m k -> p (m k)"), k_scratch[:, b, :]).then_inc(k_raw_loaded, 16)

        setup = ExitStack()
        with setup:
            ctx_raw = sb("ctx_raw", [P, RING, TT + TI], F32, setup)
            ctxT_hi = sb("ctxT_hi", [P, KC, TT + TI], F32R, setup)
            ctxT_lo = sb("ctxT_lo", [P, KC, TT + TI], F32R, setup)
            w_raw = sb("w_raw", [P, RING, D], F32, setup)
            w_hi, w_lo = (t[:].rearrange("p m q -> p (m q)").rearrange("p (r d) -> p r d", r=RING) for t in (qT_hi, qT_lo))
            k_all = sb("k_all", [P, B, KD, KEYS], F32, setup)
            k_ip = sb("k_ip", [P, D], F32, setup)
            v_text = sb("v_text", [PB, NPB, D], F32, setup)
            v_ip = sb("v_ip", [P, D], F32, setup)
            boxes = sb("boxes", [P, B * BOXES, 4], F32, setup)
            gx, gy = sb("gx", [P, 1], F32, setup), sb("gy", [P, TPB], F32, setup)
            inside_x = sb("inside_x", [P, 2, B * BOXES], F32, setup)
            inside_y = sb("inside_y", [P, 2, B * BOXES, TPB], F32, setup)
            inside = sb("inside", [P, B, BOXES, TPB], F32, setup)
            any_in = sb("any_in", [P, B, TPB], F32, setup)

            chunks = [(w, k) for w in (w_v, w_v_ip, w_k_ip, w_k) for k in range(KC)]
            KV_CHUNKS = len(chunks)
            chunks += [(w, k) for w in (w_q, w_out) for k in range(KD)]
            V0, VI0, KI0, K0 = (i * KC for i in range(4))
            WQ0, WO0 = KV_CHUNKS, KV_CHUNKS + KD

            def split_dst(c):
                if c < WQ0:
                    return w_hi[:, c % RING, :], w_lo[:, c % RING, :]
                if c < WO0:
                    return wq_hi[:, c - WQ0, :], wq_lo[:, c - WQ0, :]
                return wo_hi[:, c - WO0, :], wo_lo[:, c - WO0, :]

            ctx_loaded = [sem(f"ctx_loaded{i}") for i in range(RING)]
            w_loaded = [sem(f"w_loaded{i}") for i in range(RING)]
            ctx_hi_done, ctx_lo_done = sem("ctx_hi_done"), sem("ctx_lo_done")
            w_hi_done, w_lo_done, w_used = sem("w_hi_done"), sem("w_lo_done"), sem("w_used")
            v_text_ready, v_ip_ready, k_ip_ready, k_text_ready, k_ipT_ready = (
                sem(n) for n in ("v_text_ready", "v_ip_ready", "k_ip_ready", "k_text_ready", "k_ipT_ready"))
            v_text_act, v_text_dve = sem("v_text_act"), sem("v_text_dve")
            k_text_act, k_text_dve = sem("k_text_act"), sem("k_text_dve")
            k_ip_act, k_ip_dve = sem("k_ip_act"), sem("k_ip_dve")
            v_ip_act, v_ip_dve, k_ipT_act = sem("v_ip_act"), sem("v_ip_dve"), sem("k_ipT_act")
            mask_step, v_stored, k_stored = sem("mask_step"), sem("v_stored"), sem("k_stored")

            with nc.Block() as block:

                @block.sync
                def _(sp):
                    def load_chunk(c):
                        if c >= RING:
                            sp.wait_ge(w_lo_done, c - RING + 1)
                        w, k = chunks[c]
                        sp.dma_start(w_raw[:, c % RING, :], w[k * P:(k + 1) * P, :]).then_inc(w_loaded[c % RING], 16)

                    for k in range(KC):
                        if k >= RING:
                            sp.wait_ge(ctx_lo_done, k - RING + 1)
                        sp.dma_start(ctx_raw[:, k % RING, 0:TT], textT[k * P:(k + 1) * P, :]).then_inc(ctx_loaded[k % RING], 16)
                        sp.dma_start(ctx_raw[:, k % RING, TT:TT + TI], ipT[k * P:(k + 1) * P, :]).then_inc(ctx_loaded[k % RING], 16)
                        load_chunk(k)
                    for c in range(KC, KI0 + RING):
                        load_chunk(c)
                    v_pairs = v_scratch.rearrange("(i j) k d -> j k i d", j=2)
                    sp.wait_ge(v_text_act, NPB)
                    sp.wait_ge(v_text_dve, NPB)
                    for j in range(2):
                        sp.dma_start(v_pairs[j, 0:NTEXT, :, :], v_text[j * NTEXT:(j + 1) * NTEXT, :, :]).then_inc(v_stored, 16)
                    for c in range(KI0 + RING, K0 + RING):
                        load_chunk(c)
                    sp.wait_ge(v_ip_act, 1)
                    sp.wait_ge(v_ip_dve, 1)
                    for b in range(B):
                        sp.dma_start(v_scratch[b, NTEXT:KEYS, :], v_ip[P - TI + b * NIP:P - TI + (b + 1) * NIP, :]).then_inc(v_stored, 16)
                    for c in range(K0 + RING, len(chunks)):
                        load_chunk(c)
                    sp.wait_ge(k_ipT_act, 2)
                    sp.wait_ge(k_text_act, (KD + 1) // 2)
                    sp.wait_ge(k_text_dve, KD // 2)
                    sp.dma_start(k_scratch.rearrange("p b n -> p (b n)"), k_all[:].rearrange("p b m k -> p (b m k)")).then_inc(k_stored, 16)
                    sp.wait_ge(k_stored, 16)
                    load_k(sp, 0)
                    sp.wait_ge(v_stored, 16 * (2 + B))

                @block.gpsimd
                def _(pool):
                    nc.gpsimd.memset(ident[:], 0.0).then_inc(ident_zeroed, 1)
                    pool.wait_ge(ident_zeroed, 1)
                    nc.gpsimd.affine_select(out=ident[:], in_=ident[:], compare_op=ALU.not_equal, fill=1.0, base=0,
                                            pattern=[[-1, P]], channel_multiplier=1).then_inc(ident_made, 1)
                    def lo_chunk(c):
                        hi, lo = split_dst(c)
                        pool.wait_ge(w_hi_done, c + 1)
                        nc.gpsimd.tensor_tensor(lo, w_raw[:, c % RING, :], hi.bitcast(F32), ALU.subtract).then_inc(w_lo_done, 1)

                    for k in range(KC):
                        lo_chunk(k)
                    for c in range(KC, len(chunks)):
                        lo_chunk(c)
                        if c == K0:
                            for buf in (k_hi, k_lo):
                                nc.gpsimd.memset(buf[:].rearrange("p m j k -> p (m j k)").bitcast(F32), 0.0).then_inc(k_zeroed, 1)

                @block.scalar
                def _(act):
                    def round_chunk(c):
                        act.wait_ge(w_loaded[c % RING], 16 * (c // RING + 1))
                        if RING <= c < WQ0:
                            w, k = divmod(c - RING, KC)
                            if k == KC - 1:
                                act.wait_ge(*((v_text_ready, 2 * NPB), (v_ip_ready, 2), (k_ip_ready, 2))[w])
                            else:
                                act.wait_ge(w_used, w * (KC - 1) + k + 1)
                        nc.scalar.activation(split_dst(c)[0], w_raw[:, c % RING, :], ACT.Copy).then_inc(w_hi_done, 1)

                    for k in range(KC):
                        act.wait_ge(ctx_loaded[k % RING], 32 * (k // RING + 1))
                        nc.scalar.activation(ctxT_hi[:, k, :], ctx_raw[:, k % RING, :], ACT.Copy).then_inc(ctx_hi_done, 1)
                        round_chunk(k)
                        if k == 0:
                            act.dma_start(bias[:], b_out).then_inc(small_loaded, 16)
                            act.dma_start(boxes[:].rearrange("p n f -> p (n f)"),
                                          bbox.rearrange("(o b) m f -> o (b m f)", o=1).broadcast_to([P, B * BOXES * 4])).then_inc(small_loaded, 16)
                            act.dma_start(gx[:], grid_x).then_inc(small_loaded, 16)
                            act.dma_start(gy[:], grid_y).then_inc(small_loaded, 16)
                    for u in range(2):
                        act.dma_start(xin[:, u, :, :], x_half[u, 0]).then_inc(x_loaded[u], 16)
                    for c in range(VI0, VI0 + RING):
                        round_chunk(c)
                    for i in range(NPB):
                        act.wait_ge(v_text_ready, 2 * i + 1)
                        nc.scalar.activation(v_text[:, i, 0:HALF], bank[2 * i][0:PB, 0:HALF], ACT.Copy).then_inc(v_text_act, 1)
                    for c in range(VI0 + RING, KI0 + RING):
                        round_chunk(c)
                    act.wait_ge(v_ip_ready, 1)
                    nc.scalar.activation(v_ip[:, 0:HALF], bank[0][:, 0:HALF], ACT.Copy).then_inc(v_ip_act, 1)
                    for c in range(KI0 + RING, K0 + RING):
                        round_chunk(c)
                    act.wait_ge(k_ip_ready, 1)
                    nc.scalar.activation(k_ip[:, 0:HALF], bank[2][:, 0:HALF], ACT.Copy).then_inc(k_ip_act, 1)
                    for c in range(K0 + RING, K0 + KC):
                        round_chunk(c)
                    for n, (m0, m1) in enumerate(((0, KD - 1), (KD - 1, KD))):
                        act.wait_ge(k_ipT_ready, n + 1)
                        nc.scalar.activation(
                            k_all[:, :, m0:m1, NTEXT:KEYS].rearrange("p b m k -> p m b k"),
                            bank[n][:, 0:(m1 - m0) * P].rearrange("p (m n) -> p m n", n=P)[:, :, P - TI:P].rearrange("p m (b k) -> p m b k", b=B),
                            ACT.Copy, scale=SCALE).then_inc(k_ipT_act, 1)
                    for c in range(WQ0, WO0):
                        round_chunk(c)
                    act.wait_ge(x_loaded[0], 16)
                    for k in range(KD):
                        x_hi_part(act, 0, 0, k)
                    for m in reversed(range(0, KD, 2)):
                        act.wait_ge(k_text_ready, KD)
                        nc.scalar.activation(k_all[:, :, m, 0:NTEXT], bank[2 + m][:, 0:TT].rearrange("p (b k) -> p b k", b=B),
                                             ACT.Copy, scale=SCALE).then_inc(k_text_act, 1)
                    for m in range(KD):
                        round_chunk(WO0 + m)
                        q_hi_part(act, 0, m)
                    act.wait_ge(k_zeroed, 2)
                    k_hi_part(act, 0)

                @block.vector
                def _(dve):
                    steps = [0]

                    def step(ins):
                        ins.then_inc(mask_step, 1)
                        steps[0] += 1
                        dve.wait_ge(mask_step, steps[0])

                    def edge(f, cols=None):
                        e = boxes[:, :, f]
                        return e if cols is None else e.unsqueeze(2).broadcast_to([P, B * BOXES, cols])

                    for k in range(KC):
                        dve.wait_ge(ctx_hi_done, k + 1)
                        nc.vector.tensor_tensor(ctxT_lo[:, k, :], ctx_raw[:, k % RING, :], ctxT_hi[:, k, :].bitcast(F32), ALU.subtract).then_inc(ctx_lo_done, 1)

                    dve.wait_ge(small_loaded, 64)
                    y_all = gy[:].unsqueeze(1).broadcast_to([P, B * BOXES, TPB])
                    nc.vector.tensor_scalar(inside_x[:, 0, :], edge(0), gx[:, 0:1], None, ALU.is_le)
                    nc.vector.tensor_scalar(inside_x[:, 1, :], edge(2), gx[:, 0:1], None, ALU.is_ge)
                    nc.vector.tensor_tensor(inside_y[:, 0, :, :], y_all, edge(1, TPB), ALU.is_ge)
                    step(nc.vector.tensor_tensor(inside_y[:, 1, :, :], y_all, edge(3, TPB), ALU.is_le))
                    step(nc.vector.tensor_tensor(inside_x[:, 0, :], inside_x[:, 0, :], inside_x[:, 1, :], ALU.mult))
                    step(nc.vector.tensor_tensor(inside_y[:, 0, :, :], inside_y[:, 0, :, :], inside_y[:, 1, :, :], ALU.mult))
                    ins_all = inside[:].rearrange("p b m t -> p (b m) t")
                    step(nc.vector.tensor_tensor(ins_all, inside_y[:, 0, :, :], inside_x[:, 0, :].unsqueeze(2).broadcast_to([P, B * BOXES, TPB]), ALU.mult))
                    step(nc.vector.tensor_reduce(any_in[:], inside[:].rearrange("p b m t -> p b t m"), AX.X, ALU.max))
                    mask_b = mask[:].rearrange("p (b t) k -> p b t k", b=B)
                    for n in range(BOXES):
                        nc.vector.tensor_scalar(mask_b[:, :, :, n], any_in[:], NEG, None, ALU.mult)
                        last = nc.vector.tensor_scalar(mask_b[:, :, :, BOXES + n], inside[:, :, n, :], 1.0, -NEG, ALU.subtract, ALU.mult)
                    step(last)

                    for i in range(NPB):
                        dve.wait_ge(v_text_ready, 2 * i + 2)
                        nc.vector.tensor_copy(v_text[:, i, HALF:D], bank[2 * i + 1][0:PB, 0:HALF]).then_inc(v_text_dve, 1)
                    dve.wait_ge(v_ip_ready, 2)
                    nc.vector.tensor_copy(v_ip[:, HALF:D], bank[1][:, 0:HALF]).then_inc(v_ip_dve, 1)
                    dve.wait_ge(k_ip_ready, 2)
                    nc.vector.tensor_copy(k_ip[:, HALF:D], bank[3][:, 0:HALF]).then_inc(k_ip_dve, 1)
                    for k in range(KD):
                        x_lo_part(dve, 0, 0, k)
                    for m in range(1, KD, 2):
                        dve.wait_ge(k_text_ready, m + 1)
                        nc.vector.tensor_scalar(k_all[:, :, m, 0:NTEXT], bank[2 + m][:, 0:TT].rearrange("p (b k) -> p b k", b=B),
                                                SCALE, None, ALU.mult).then_inc(k_text_dve, 1)
                    for m in range(KD):
                        q_lo_part(dve, 0, m)
                    k_lo_part(dve, 0)

                @block.tensor
                def _(pe):
                    def tokens_times_w(c, toks, h, dst, first, last):
                        k, s, cols = c % KC, c % RING, slice(h * HALF, (h + 1) * HALF)
                        return three(dst, ctxT_hi[:, k, toks], ctxT_lo[:, k, toks], w_hi[:, s, cols], w_lo[:, s, cols], first, last)

                    for k in range(KC):
                        pe.wait_ge(ctx_lo_done, k + 1)
                        pe.wait_ge(w_lo_done, V0 + k + 1)
                        for n in range(2 * NPB):
                            i, h = n // 2, n % 2
                            ins = tokens_times_w(V0 + k, slice(i * PB, (i + 1) * PB), h, bank[n][0:PB, 0:HALF], k == 0, k == KC - 1)
                            if k == KC - 1:
                                ins.then_inc(v_text_ready, 1)
                        if k < KC - 1:
                            ins.then_inc(w_used, 1)
                    ip_toks = slice(TT + TI - P, TT + TI)
                    for c0, b0, ready in ((VI0, 0, v_ip_ready), (KI0, 2, k_ip_ready)):
                        for k in range(KC):
                            pe.wait_ge(w_lo_done, c0 + k + 1)
                            for h in range(2):
                                if k == 0:
                                    pe.wait_ge(v_text_dve if h else v_text_act, b0 // 2 + 1)
                                ins = tokens_times_w(c0 + k, ip_toks, h, bank[b0 + h][:, 0:HALF], k == 0, k == KC - 1)
                                if k == KC - 1:
                                    ins.then_inc(ready, 1)
                            if k < KC - 1:
                                ins.then_inc(w_used, 1)
                    pe.wait_ge(ident_made, 1)
                    for k in range(KC):
                        pe.wait_ge(w_lo_done, K0 + k + 1)
                        s = (K0 + k) % RING
                        for m in reversed(range(KD)) if k == 0 else range(KD):
                            if k == 0 and m < 2:
                                pe.wait_ge(k_ip_dve if m else k_ip_act, 1)
                            if k == 0 and m >= 2:
                                pe.wait_ge(v_text_dve if m % 2 else v_text_act, (2 + m) // 2 + 1)
                            rows = slice(m * P, (m + 1) * P)
                            ins = three(bank[2 + m][:, 0:TT], w_hi[:, s, rows], w_lo[:, s, rows], ctxT_hi[:, k, 0:TT], ctxT_lo[:, k, 0:TT],
                                        k == 0, k == KC - 1)
                            if k == KC - 1:
                                ins.then_inc(k_text_ready, 1)
                        if k < KC - 1:
                            ins.then_inc(w_used, 1)
                        if k == 0:
                            pe.wait_ge(v_ip_act, 1)
                            pe.wait_ge(v_ip_dve, 1)
                            for m in range(KD):
                                ins = nc.tensor.transpose(bank[m // (KD - 1)][:, m % (KD - 1) * P:(m % (KD - 1) + 1) * P], k_ip[:, m * P:(m + 1) * P], ident[:])
                                if m >= KD - 2:
                                    ins.then_inc(k_ipT_ready, 1)
                    pe.wait_ge(w_lo_done, WQ0 + KD)
                    for m in range(KD):
                        if m == 0:
                            pe.wait_ge(v_text_dve, NPB)
                        elif m == 1:
                            pe.wait_ge(k_text_act, 1)
                        else:
                            pe.wait_ge(q_lo_done, m - 1)
                        q_steps(pe, 0, m)

        res = sb("res", [P, 2, KD, GQ])
        prob = sb("prob", [P, GT * SW])
        pT_hi, pT_lo = sb("pT_hi", [P, 2, GQ], F32R), sb("pT_lo", [P, 2, GQ], F32R)
        pv_part = sb("pv_part", [P, GQ])
        o_raw = sb("o_raw", [P, 2, GQ])
        oT_hi, oT_lo = sb("oT_hi", [P, KD, GQ], F32R), sb("oT_lo", [P, KD, GQ], F32R)
        v_raw = sb("v_raw", [P, D])
        v_parts = sb("v_parts", [P, PAIRS, 2, HP], F32R)
        top, total, inv = sb("top", [P, GT, 2, HEADS]), sb("total", [P, GT, 2, HEADS]), sb("inv", [P, GT, 2, HEADS])

        s_bank, t_bank, v_bank = bank[0:4], bank[2:4], bank[4:6]

        v_raw_loaded, v_zeroed, v_hi_built, v_built = (sem(n) for n in ("v_raw_loaded", "v_zeroed", "v_hi_built", "v_built"))
        score_ready, pT_ready, pv_ready, out_ready = (sem(n) for n in ("score_ready", "pT_ready", "pv_ready", "out_ready"))
        score_copied, exp_done, res_done, pT_hi_done, pv_moved, oT_hi_done = (
            sem(n) for n in ("score_copied", "exp_done", "res_done", "pT_hi_done", "pv_moved", "oT_hi_done"))
        max_done, sum_done, inv_done, pT_lo_done, pv_added, out_done = (
            sem(n) for n in ("max_done", "sum_done", "inv_done", "pT_lo_done", "pv_added", "out_done"))
        mask_added, max_subbed, prob_done, oT_lo_done = (sem(n) for n in ("mask_added", "max_subbed", "prob_done", "oT_lo_done"))
        stored = [sem("stored0"), sem("stored1")]

        def units_for_tile(t):
            return -(-(t + 1) * SW // 512)

        def tile(t):
            return prob[:, t * SW:(t + 1) * SW].rearrange("p (h k) -> p h k", k=KEYS)

        def own_rows(p):
            return (slice(0, HP), slice(HP, P)) if p % 2 == 0 else (slice(HP, P), slice(0, HP))

        def q_ahead(before):
            return 2 if before else 4

        def q_slot(s, before):
            rest = KD - q_ahead(before)
            return [(q_ahead(before) + i // KD, i % KD) for i in range(s * rest, (s + 1) * rest)]

        def q_finished(s, before):
            return [m for m, k in q_slot(s, before) if k == KD - 1]

        def v_head(t, part, j):
            return t[j * HP:(j + 1) * HP, :, part, j * DH:(j + 1) * DH]

        def v_own(j):
            return v_raw[j * HP:(j + 1) * HP, :].rearrange("p (n c) -> p n c", n=PAIRS)[:, :, j * DH:(j + 1) * DH]

        SPANS = ((0, NTEXT), (NTEXT, KEYS))

        with nc.Block() as block:

            @block.sync
            def _(sp):
                def load_v(b):
                    wait(sp, v_built, 2 * b)
                    for h in range(2):
                        sp.dma_start(v_raw[h * KEYS:(h + 1) * KEYS, :], v_scratch[b]).then_inc(v_raw_loaded, 16)

                def group(g, u, b, stores, loads):
                    if loads and u == 0:
                        sp.wait_ge(k_built, HPT * (b + 1))
                        load_k(sp, b + 1)
                    if loads and u == 1:
                        load_v(b + 1)
                    if loads:
                        sp.wait_ge(res_done, KD * (g + 1))
                        sp.wait_ge(xT_lo_done, KD * (g + 1))
                        sp.dma_start(xin[:, u, :, :], x_half[u, b + 1]).then_inc(x_loaded[u], 16)
                    if stores:
                        for m in range(KD):
                            store(g - 1, 1 - u, b if u else b - 1, m)

                def store(g, u, b, m):
                    sp.wait_ge(out_done, KD * g + m + 1)
                    sp.dma_start(out_half[u, b, m], res[:, u, m, :]).then_inc(stored[u], 16)

                load_v(0)
                group(0, 0, 0, False, True)
                group(1, 1, 0, True, True)
                with sp.Fori(1, B - 1) as b:
                    group(2 * b, 0, b, True, True)
                    group(2 * b + 1, 1, b, True, True)
                group(NG - 2, 0, B - 1, True, False)
                group(NG - 1, 1, B - 1, True, False)
                for m in range(KD):
                    store(NG - 1, 1, B - 1, m)
                for u in range(2):
                    sp.wait_ge(stored[u], 16 * KD * NG // 2)

            @block.gpsimd
            def _(pool):
                def add_mask(g, t):
                    pool.wait_ge(score_copied, UNITS * g + units_for_tile(t))
                    ip = tile(t)[:, :, NTEXT:KEYS]
                    m = mask[:, GT * g + t, :].unsqueeze(1).broadcast_to([P, HEADS, NIP])
                    nc.gpsimd.tensor_tensor(ip, ip, m, ALU.add).then_inc(mask_added, 1)

                def sub_max(g, t):
                    pool.wait_ge(max_done, GT * g + t + 1)
                    for n, (k0, k1) in enumerate(SPANS):
                        s = tile(t)[:, :, k0:k1]
                        m = top[:, t, n, :].unsqueeze(2).broadcast_to([P, HEADS, k1 - k0])
                        ins = nc.gpsimd.tensor_tensor(s, s, m, ALU.subtract)
                    ins.then_inc(max_subbed, 1)

                def normalise(g, t):
                    pool.wait_ge(inv_done, GT * g + t + 1)
                    for n, (k0, k1) in enumerate(SPANS):
                        s = tile(t)[:, :, k0:k1]
                        r = inv[:, t, n, :].unsqueeze(2).broadcast_to([P, HEADS, k1 - k0])
                        ins = nc.gpsimd.tensor_tensor(s, s, r, ALU.mult)
                    ins.then_inc(prob_done, 1)

                def oT_part(g, m):
                    pool.wait_ge(oT_hi_done, KD * g + m + 1)
                    nc.gpsimd.tensor_tensor(oT_lo[:, m, :], o_raw[:, m % 2, :], oT_hi[:, m, :].bitcast(F32), ALU.subtract).then_inc(oT_lo_done, 1)

                def group(g, before):
                    add_mask(g, 0)
                    if before:
                        oT_part(g - 1, KD - 1)
                    add_mask(g, 1)
                    add_mask(g, 2)
                    sub_max(g, 0)
                    add_mask(g, 3)
                    for t in range(1, GT):
                        sub_max(g, t)
                    for t in range(GT):
                        normalise(g, t)
                    for m in range(KD - 1):
                        oT_part(g, m)

                nc.gpsimd.memset(v_parts[:].rearrange("p n s c -> p (n s c)").bitcast(F32), 0.0).then_inc(v_zeroed, 1)
                group(0, False)
                group(1, True)
                with pool.Fori(1, B - 1) as b:
                    group(2 * b, True)
                    group(2 * b + 1, True)
                group(NG - 2, True)
                group(NG - 1, True)
                oT_part(NG - 1, KD - 1)

            @block.scalar
            def _(act):
                def copy_scores(g, u):
                    act.wait_ge(score_ready, UNITS * g + u + 1)
                    nc.scalar.activation(prob[:, u * 512:(u + 1) * 512], s_bank[u % 4][:], ACT.Copy).then_inc(score_copied, 1)

                def exponentials(g, t):
                    act.wait_ge(max_subbed, GT * g + t + 1)
                    nc.scalar.activation(prob[:, t * SW:(t + 1) * SW], prob[:, t * SW:(t + 1) * SW], ACT.Exp).then_inc(exp_done, 1)

                def pT_part(g, p):
                    act.wait_ge(pT_ready, PAIRS * g + p + 1)
                    nc.scalar.activation(pT_hi[:, p % 2, :], t_bank[p % 2][:], ACT.Copy).then_inc(pT_hi_done, 1)

                def move_pv(g, p):
                    act.wait_ge(pv_ready, PAIRS * g + p + 1)
                    own, other = own_rows(p)
                    nc.scalar.activation(pv_part[own, :], v_bank[p % 2][other, :], ACT.Copy).then_inc(pv_moved, 1)

                def oT_part(g, m):
                    act.wait_ge(pv_added, PAIRS * g + 2 * m + 2)
                    nc.scalar.activation(oT_hi[:, m, :], o_raw[:, m % 2, :], ACT.Copy).then_inc(oT_hi_done, 1)

                def residual(g, u, b, m):
                    if m == 0:
                        wait(act, x_loaded[u], 16 * (b + 1))
                        wait(act, stored[u], 16 * KD * b)
                    nc.scalar.activation(res[:, u, m, :], xin[:, u, m, :], ACT.Identity, bias=bias[:, m:m + 1]).then_inc(res_done, 1)

                def v_hi_part(b):
                    act.wait_ge(v_zeroed, 1)
                    act.wait_ge(v_raw_loaded, 32 * (b + 1))
                    wait(act, pv_ready, PAIRS * GPB * b)
                    for j in range(2):
                        nc.scalar.activation(v_head(v_parts, 0, j), v_own(j), ACT.Copy).then_inc(v_hi_built, 1)

                def group(g, u, b, before, more):
                    def split_x(k0, k1):
                        if more:
                            if k0 == 0:
                                act.wait_ge(x_loaded[1 - u], 16 * (b + u + 1))
                                act.wait_ge(q_ready, KD * (g + 1))
                            for k in range(k0, k1):
                                x_hi_part(act, g + 1, 1 - u, k)

                    if not before:
                        split_x(0, KD)
                    for n in range(UNITS):
                        copy_scores(g, n)
                        if n == 1 and before:
                            oT_part(g - 1, KD - 1)
                    if before:
                        split_x(0, 3)
                    for t in range(GT):
                        exponentials(g, t)
                        if before and t == 0:
                            split_x(3, KD)
                        if not before and more and t > 0 and t < 3:
                            q_hi_part(act, g + 1, t - 1)
                    for m in range(KD):
                        residual(g, u, b, m)
                    if u == 0:
                        v_hi_part(b)
                    elif more:
                        act.wait_ge(score_ready, UNITS * (g + 1))
                        k_hi_part(act, b + 1)
                    if more:
                        for m in range(0 if before else 2, q_ahead(before)):
                            q_hi_part(act, g + 1, m)
                    for s in range(KD):
                        pT_part(g, 2 * s)
                        pT_part(g, 2 * s + 1)
                        if s:
                            oT_part(g, s - 1)
                        if more:
                            for m in q_finished(s, before):
                                q_hi_part(act, g + 1, m)
                        move_pv(g, 2 * s)
                        move_pv(g, 2 * s + 1)

                group(0, 0, 0, False, True)
                group(1, 1, 0, True, True)
                with act.Fori(1, B - 1) as b:
                    group(2 * b, 0, b, True, True)
                    group(2 * b + 1, 1, b, True, True)
                group(NG - 2, 0, B - 1, True, True)
                group(NG - 1, 1, B - 1, True, False)
                oT_part(NG - 1, KD - 1)

            @block.vector
            def _(dve):
                def pT_part(g, p):
                    dve.wait_ge(pT_hi_done, PAIRS * g + p + 1)
                    nc.vector.tensor_tensor(pT_lo[:, p % 2, :], t_bank[p % 2][:], pT_hi[:, p % 2, :].bitcast(F32), ALU.subtract).then_inc(pT_lo_done, 1)

                def add_pv(g, p):
                    m, own = p // 2, own_rows(p)[0]
                    if p % 2 == 0:
                        wait(dve, oT_lo_done, KD * g + max(m - 1, 0))
                    dve.wait_ge(pv_moved, PAIRS * g + p + 1)
                    nc.vector.tensor_tensor(o_raw[own, m % 2, :], v_bank[p % 2][own, :], pv_part[own, :], ALU.add).then_inc(pv_added, 1)

                def maxima(g, t):
                    dve.wait_ge(mask_added, GT * g + t + 1)
                    for n, (k0, k1) in enumerate(SPANS):
                        ins = nc.vector.tensor_reduce(top[:, t, n, :], tile(t)[:, :, k0:k1], AX.X, ALU.max)
                    ins.then_inc(max_done, 1)

                def sums(g, t):
                    dve.wait_ge(exp_done, GT * g + t + 1)
                    for n, (k0, k1) in enumerate(SPANS):
                        nc.vector.tensor_reduce(total[:, t, n, :], tile(t)[:, :, k0:k1], AX.X, ALU.add).then_inc(sum_done, 1)
                    dve.wait_ge(sum_done, 2 * (GT * g + t + 1))
                    nc.vector.reciprocal(inv[:, t, :, :], total[:, t, :, :]).then_inc(inv_done, 1)

                def output(g, u, m):
                    if m == 0:
                        dve.wait_ge(res_done, KD * (g + 1))
                    dve.wait_ge(out_ready, KD * g + m + 1)
                    r = res[:, u, m, :]
                    nc.vector.tensor_tensor(r, l_bank[m % 2][:], r, ALU.add).then_inc(out_done, 1)

                def v_lo_part(b):
                    for j in range(2):
                        dve.wait_ge(v_hi_built, 2 * b + j + 1)
                        nc.vector.tensor_tensor(v_head(v_parts, 1, j), v_own(j), v_head(v_parts, 0, j).bitcast(F32), ALU.subtract).then_inc(v_built, 1)

                def group(g, u, b, before, more):
                    def split_x(k0, k1):
                        if more:
                            for k in range(k0, k1):
                                x_lo_part(dve, g + 1, 1 - u, k)

                    if not before:
                        split_x(0, KD)
                    for t in range(GT):
                        maxima(g, t)
                        if before and t == 2:
                            split_x(0, 2)
                    if before:
                        output(g - 1, 1 - u, 0)
                    for t in range(GT):
                        if before and t < 3:
                            split_x(t + 2, t + 3)
                        sums(g, t)
                        if before:
                            output(g - 1, 1 - u, t + 1)
                        if not before and more and t > 0 and t < 3:
                            q_lo_part(dve, g + 1, t - 1)
                    if u == 0:
                        v_lo_part(b)
                    elif more:
                        k_lo_part(dve, b + 1)
                    if more:
                        for m in range(0 if before else 2, q_ahead(before)):
                            q_lo_part(dve, g + 1, m)
                    for s in range(KD):
                        pT_part(g, 2 * s)
                        pT_part(g, 2 * s + 1)
                        if more:
                            for m in q_finished(s, before):
                                q_lo_part(dve, g + 1, m)
                        add_pv(g, 2 * s)
                        add_pv(g, 2 * s + 1)

                group(0, 0, 0, False, True)
                group(1, 1, 0, True, True)
                with dve.Fori(1, B - 1) as b:
                    group(2 * b, 0, b, True, True)
                    group(2 * b + 1, 1, b, True, True)
                group(NG - 2, 0, B - 1, True, True)
                group(NG - 1, 1, B - 1, True, False)
                for m in range(KD):
                    output(NG - 1, 1, m)

            @block.tensor
            def _(pe):
                def score_unit(g, n, b, new_batch):
                    if n < 2:
                        wait(pe, score_copied, UNITS * g)
                    elif n < 4:
                        wait(pe, pT_lo_done, PAIRS * g)
                    else:
                        pe.wait_ge(score_copied, UNITS * g + n - 3)
                    if n == 0 and new_batch:
                        pe.wait_ge(k_built, HPT * (b + 1))
                    for half in range(2):
                        t, m = divmod(2 * n + half, KD)
                        if t == 0:
                            pe.wait_ge(q_lo_done, KD * g + m + 1)
                        q_cols = slice(t * P, (t + 1) * P)
                        keys = [k[:, m, :, :].rearrange("p j k -> p (j k)") for k in (k_hi, k_lo)]
                        ins = three(s_bank[n % 4][:, half * CW:(half + 1) * CW], qT_hi[:, m, q_cols], qT_lo[:, m, q_cols], *keys, True, True)
                    ins.then_inc(score_ready, 1)

                def p_transpose(g, p):
                    if p < 2:
                        pe.wait_ge(score_copied, UNITS * (g + 1))
                    else:
                        pe.wait_ge(pT_lo_done, PAIRS * g + p - 1)
                    for t in range(GT):
                        if p == 0:
                            pe.wait_ge(prob_done, GT * g + t + 1)
                        src = prob[:, t * SW + p * P:t * SW + (p + 1) * P]
                        ins = nc.tensor.transpose(t_bank[p % 2][:, t * P:(t + 1) * P], src, ident[:])
                    ins.then_inc(pT_ready, 1)

                def pv_pair(g, p, b, new_batch):
                    if p == 0 and new_batch:
                        pe.wait_ge(v_built, 2 * (b + 1))
                    wait(pe, pv_added, PAIRS * g + max(p - 1, 0))
                    pe.wait_ge(pT_lo_done, PAIRS * g + p + 1)
                    v = v_parts[:, p, :, :].rearrange("p s c -> p (s c)")
                    nc.tensor.matmul(v_bank[p % 2][:], v, pT_hi[:, p % 2, :], start=True, stop=False)
                    nc.tensor.matmul(v_bank[p % 2][:], v, pT_lo[:, p % 2, :], start=False, stop=True).then_inc(pv_ready, 1)

                def out_tile(g, m, more=True):
                    if m >= 2:
                        pe.wait_ge(out_done, KD * g + m - 1)
                    elif more:
                        pe.wait_ge(q_lo_done, KD * (g + 2))
                    else:
                        pe.wait_ge(out_done, KD * g)
                    cols = slice(m * P, (m + 1) * P)
                    for k in range(KD):
                        if m == 0:
                            pe.wait_ge(oT_lo_done, KD * g + k + 1)
                        ins = three(l_bank[m % 2][:], wo_hi[:, k, cols], wo_lo[:, k, cols], oT_hi[:, k, :], oT_lo[:, k, :], k == 0, k == KD - 1)
                    ins.then_inc(out_ready, 1)

                def group(g, b, new_batch, before, more):
                    for n in range(UNITS):
                        score_unit(g, n, b, new_batch)
                    if before:
                        for m in range(KD):
                            out_tile(g - 1, m)
                    if more:
                        for m in range(q_ahead(before)):
                            if m < 2:
                                wait(pe, out_done, KD * g - (1 if m == 0 else 0))
                            else:
                                pe.wait_ge(q_lo_done, KD * (g + 1) + m - 1)
                            q_steps(pe, g + 1, m)
                    for s in range(KD):
                        p_transpose(g, 2 * s)
                        p_transpose(g, 2 * s + 1)
                        if more:
                            for m, k in q_slot(s, before):
                                if k == 0:
                                    pe.wait_ge(q_lo_done, KD * (g + 1) + m - 1)
                                q_steps(pe, g + 1, m, k, k + 1)
                        pv_pair(g, 2 * s, b, new_batch)
                        pv_pair(g, 2 * s + 1, b, new_batch)

                group(0, 0, True, False, True)
                group(1, 0, False, True, True)
                with pe.Fori(1, B - 1) as b:
                    group(2 * b, b, True, True, True)
                    group(2 * b + 1, b, False, True, True)
                group(NG - 2, B - 1, True, True, True)
                group(NG - 1, B - 1, False, True, False)
                for m in range(KD):
                    out_tile(NG - 1, m, more=False)


_WEIGHTS = ["L0_xattn_w_q", "L0_xattn_w_k", "L0_xattn_w_v", "L0_xattn_w_k_ip", "L0_xattn_w_v_ip", "L0_xattn_w_out"]


def kernel(**inputs):
    import numpy as np
    import concourse.bacc as bacc
    from concourse.bass_utils import run_bass_kernel_spmd

    x, ctx = np.asarray(inputs["x"]), np.asarray(inputs["ctx_2048"])
    width, seq = ctx.shape[2], x.shape[1]
    text = ctx.shape[1] - NIP
    line = np.arange(GRID, dtype=np.float32) * np.float32(1.0 / (GRID - 1))
    n = np.arange(seq).reshape(seq // P, P).T
    laid_out = {
        "xT": x.transpose(0, 2, 1),
        "textT": ctx[:, :text].transpose(2, 0, 1).reshape(width, -1),
        "ipT": ctx[:, text:].transpose(2, 0, 1).reshape(width, -1),
        "bbox": np.asarray(inputs["fside_Bx4x4_0"]),
        **{w: np.asarray(inputs[w]) for w in _WEIGHTS},
        "b_out": np.asarray(inputs["L0_xattn_b_out"]).reshape(-1, P).T,
        "grid_x": line[n[:, 0:1] % GRID],
        "grid_y": line[n // GRID],
    }
    nc = bacc.Bacc("TRN2", target_bir_lowering=False, num_devices=1)
    arrays, args = {}, []
    for name, a in laid_out.items():
        a = np.ascontiguousarray(a)
        arrays[f"in_{name}"] = a
        args.append(nc.dram_tensor(f"in_{name}", a.shape, mybir.dt.from_np(a.dtype), kind="ExternalInput").ap())
    args.append(nc.dram_tensor("outT", (x.shape[0], x.shape[2], x.shape[1]), F32, kind="ExternalOutput").ap())
    attention_kernel(nc, *args)
    r = run_bass_kernel_spmd(nc, [arrays], core_ids=[0])
    return np.ascontiguousarray(r.results[0]["outT"].transpose(0, 2, 1))
```

```python
from contextlib import ExitStack

import concourse.bass as bass
from concourse import mybir

F32 = mybir.dt.float32
F32R = mybir.dt.float32r
ACT = mybir.ActivationFunctionType
ALU = mybir.AluOpType
AX = mybir.AxisListType

P = 128
HEADS, DH = 20, 32
NIP = 8
BOXES = 4
NEG = -10000.0
GRID = 32
GQ = 512
GT = GQ // P
RING = 4
LOADS = 6


def attention_kernel(nc, xT_dram, textT, ipT, bbox, w_q, w_k, w_v, w_k_ip, w_v_ip, w_out, b_out, grid_x, grid_y, outT):
    B, D, S = xT_dram.shape
    C, TT = textT.shape
    TI = ipT.shape[1]
    NTEXT = TT // B
    KEYS = NTEXT + NIP
    KD, KC = D // P, C // P
    GPB = S // GQ
    NG = B * GPB
    TPB = S // P
    HPT = P // DH
    PAIRS = HEADS // 2
    HP = P // 2
    CW = HPT * KEYS
    SW = HEADS * KEYS
    UNITS = GT * SW // 512
    HALF = D // 2
    PB = 2 * NTEXT
    NPB = B // 2
    SCALE = float(DH) ** -0.5

    x_half = xT_dram.rearrange("b (k p) (h q) -> h b p k q", p=P, q=GQ)
    out_half = outT.rearrange("b (m p) (h q) -> h b m p q", p=P, q=GQ)
    k_scratch = nc.dram_tensor("k_scratch", (P, B, KD * KEYS), F32).ap()
    v_scratch = nc.dram_tensor("v_scratch", (B, KEYS, D), F32).ap()

    whole = ExitStack()
    with whole:
        def sb(name, shape, dt=F32, stack=whole):
            return stack.enter_context(nc.sbuf_tensor(name, shape, dt))

        def sem(name):
            return whole.enter_context(nc.semaphore(name))

        bank = [whole.enter_context(nc.psum_tensor(f"bank{i}", [P, 512], F32)) for i in range(8)]

        ident = sb("ident", [P, P])
        wq_hi, wq_lo = sb("wq_hi", [P, KD, D], F32R), sb("wq_lo", [P, KD, D], F32R)
        wo_hi, wo_lo = sb("wo_hi", [P, KD, D], F32R), sb("wo_lo", [P, KD, D], F32R)
        xin = sb("xin", [P, 2, KD, GQ])
        xT_hi, xT_lo = sb("xT_hi", [P, KD * GQ], F32R), sb("xT_lo", [P, KD * GQ], F32R)
        qT_hi, qT_lo = sb("qT_hi", [P, KD, GQ], F32R), sb("qT_lo", [P, KD, GQ], F32R)
        k_hi, k_lo = sb("k_hi", [P, KD, HPT, KEYS], F32R), sb("k_lo", [P, KD, HPT, KEYS], F32R)
        k_raw = sb("k_raw", [P, KD, KEYS])
        mask = sb("mask", [P, B * TPB, NIP])
        bias = sb("bias", [P, KD])

        x_loaded = [sem("x_loaded0"), sem("x_loaded1")]
        small_loaded, ident_zeroed, ident_made = sem("small_loaded"), sem("ident_zeroed"), sem("ident_made")
        xT_hi_done, xT_lo_done = sem("xT_hi_done"), sem("xT_lo_done")
        q_ready, q_hi_done, q_lo_done = sem("q_ready"), sem("q_hi_done"), sem("q_lo_done")
        k_zeroed, k_raw_loaded, k_hi_built, k_built = (sem(n) for n in ("k_zeroed", "k_raw_loaded", "k_hi_built", "k_built"))

        l_bank = bank[6:8]

        def wait(eng, s, value):
            if not (isinstance(value, int) and value <= 0):
                eng.wait_ge(s, value)

        def three(dst, a_hi, a_lo, b_hi, b_lo, first, last):
            nc.tensor.matmul(dst, a_hi, b_hi, start=first, stop=False)
            nc.tensor.matmul(dst, a_hi, b_lo, start=False, stop=False)
            return nc.tensor.matmul(dst, a_lo, b_hi, start=False, stop=last)


        def x_tile(t, k):
            return t[:, k * GQ:(k + 1) * GQ]

        def x_hi_part(act, g, u, k):
            nc.scalar.activation(x_tile(xT_hi, k), xin[:, u, k, :], ACT.Copy).then_inc(xT_hi_done, 1)

        def x_lo_part(dve, g, u, k):
            dve.wait_ge(xT_hi_done, KD * g + k + 1)
            nc.vector.tensor_tensor(x_tile(xT_lo, k), xin[:, u, k, :], x_tile(xT_hi, k).bitcast(F32), ALU.subtract).then_inc(xT_lo_done, 1)

        def q_steps(pe, g, m, k0=0, k1=KD):
            cols = slice(m * P, (m + 1) * P)
            for k in range(k0, k1):
                if m == 0:
                    pe.wait_ge(xT_lo_done, KD * g + k + 1)
                ins = three(l_bank[(m + 1) % 2][:], wq_hi[:, k, cols], wq_lo[:, k, cols], x_tile(xT_hi, k), x_tile(xT_lo, k), k == 0, k == KD - 1)
            if k1 == KD:
                ins.then_inc(q_ready, 1)

        def q_hi_part(act, g, m):
            act.wait_ge(q_ready, KD * g + m + 1)
            nc.scalar.activation(qT_hi[:, m, :], l_bank[(m + 1) % 2][:], ACT.Copy).then_inc(q_hi_done, 1)

        def q_lo_part(dve, g, m):
            dve.wait_ge(q_hi_done, KD * g + m + 1)
            nc.vector.tensor_tensor(qT_lo[:, m, :], l_bank[(m + 1) % 2][:], qT_hi[:, m, :].bitcast(F32), ALU.subtract).then_inc(q_lo_done, 1)

        def k_head(t, j):
            return t[j * DH:(j + 1) * DH, :, j, :]

        def k_hi_part(act, b):
            act.wait_ge(k_raw_loaded, 16 * (b + 1))
            for j in range(HPT):
                nc.scalar.activation(k_head(k_hi, j), k_raw[j * DH:(j + 1) * DH, :, :], ACT.Copy).then_inc(k_hi_built, 1)

        def k_lo_part(dve, b):
            for j in range(HPT):
                dve.wait_ge(k_hi_built, HPT * b + j + 1)
                nc.vector.tensor_tensor(k_head(k_lo, j), k_raw[j * DH:(j + 1) * DH, :, :], k_head(k_hi, j).bitcast(F32), ALU.subtract).then_inc(k_built, 1)

        def load_k(sp, b):
            sp.dma_start(k_raw[:].rearrange("p m k -> p (m k)"), k_scratch[:, b, :]).then_inc(k_raw_loaded, 16)

        setup = ExitStack()
        with setup:
            ctx_raw = sb("ctx_raw", [P, RING, TT + TI], F32, setup)
            ctxT_hi = sb("ctxT_hi", [P, KC, TT], F32R, setup)
            ctxT_lo = sb("ctxT_lo", [P, KC, TT], F32R, setup)
            ipT_parts = sb("ipT_parts", [P, KC, 2, TI], F32R, setup)
            w_raw = sb("w_raw", [P, LOADS, D], F32, setup)
            w_hi, w_lo = (t[:].rearrange("p m q -> p (m q)").rearrange("p (r d) -> p r d", r=RING) for t in (qT_hi, qT_lo))
            k_all = sb("k_all", [P, B, KD, KEYS], F32, setup)
            k_ip, v_ip = sb("k_ip", [TI, D], F32, setup), sb("v_ip", [TI, D], F32, setup)
            ip_part = ctx_raw[0:TI].rearrange("p r t -> p (r t)")
            v_text = sb("v_text", [PB, NPB, D], F32, setup)
            boxes = sb("boxes", [P, B * BOXES, 4], F32, setup)
            gx, gy = sb("gx", [P, 1], F32, setup), sb("gy", [P, TPB], F32, setup)
            inside_x = sb("inside_x", [P, 2, B * BOXES], F32, setup)
            inside_y = sb("inside_y", [P, 2, B * BOXES, TPB], F32, setup)
            inside = sb("inside", [P, B, BOXES, TPB], F32, setup)
            any_in = sb("any_in", [P, B, TPB], F32, setup)

            chunks, ring_place = [], []

            def stream(name, k, ring=True):
                ring_place.append(len([r for r in ring_place if r is not None]) if ring else None)
                chunks.append((name, k))

            for k in range(KC):
                stream("v", k)
            for k in range(KC):
                stream("k", k)
                place = KC + 3 * k + 1
                for name in ("v_ip", "k_ip") if place % RING < (place + 1) % RING else ("k_ip", "v_ip"):
                    stream(name, k)
                if 0 < k <= KD:
                    stream("q", k - 1, False)
            for k in range(KD):
                stream("out", k, False)
            weights = {"v": w_v, "k": w_k, "v_ip": w_v_ip, "k_ip": w_k_ip, "q": w_q, "out": w_out}
            WO0 = chunks.index(("out", 0))

            def slot(name, k):
                return ring_place[chunks.index((name, k))] % RING

            def split_dst(c):
                name, k = chunks[c]
                if name == "q":
                    return wq_hi[:, k, :], wq_lo[:, k, :]
                if name == "out":
                    return wo_hi[:, k, :], wo_lo[:, k, :]
                return w_hi[:, ring_place[c] % RING, :], w_lo[:, ring_place[c] % RING, :]

            ctx_loaded = [sem(f"ctx_loaded{i}") for i in range(RING)]
            w_loaded = [sem(f"w_loaded{i}") for i in range(LOADS)]
            ctx_hi_done, ctx_lo_done = sem("ctx_hi_done"), sem("ctx_lo_done")
            w_hi_done, w_used = sem("w_hi_done"), sem("w_used")
            w_lo_done = [sem("w_lo_done_dve"), sem("w_lo_done_pool")]
            v_text_ready, k_text_ready, ip_ready, k_ipT_ready = (sem(n) for n in ("v_text_ready", "k_text_ready", "ip_ready", "k_ipT_ready"))
            v_text_act, v_text_dve = sem("v_text_act"), sem("v_text_dve")
            k_text_act, k_text_dve, k_ipT_act = sem("k_text_act"), sem("k_text_dve"), sem("k_ipT_act")
            ip_moved, ip_added = sem("ip_moved"), sem("ip_added")
            mask_step, v_stored, k_stored = sem("mask_step"), sem("v_stored"), sem("k_stored")

            def wait_lo(eng, name, k):
                c = chunks.index((name, k))
                eng.wait_ge(w_lo_done[c % 2], c // 2 + 1)

            REST = D - 512
            IP_BANKS = ((1, 0, 512), (7, 512, 512 + 2 * REST), (0, 512 + 2 * REST, 2 * D))

            with nc.Block() as block:

                @block.sync
                def _(sp):
                    def load_chunk(c):
                        if c >= LOADS:
                            wait_lo(sp, *chunks[c - LOADS])
                        name, k = chunks[c]
                        sp.dma_start(w_raw[:, c % LOADS, :], weights[name][k * P:(k + 1) * P, :]).then_inc(w_loaded[c % LOADS], 16)

                    for k in range(KC):
                        load_chunk(k)
                        if k >= RING:
                            sp.wait_ge(ctx_lo_done, k - RING + 1)
                        sp.dma_start(ctx_raw[:, k % RING, 0:TT], textT[k * P:(k + 1) * P, :]).then_inc(ctx_loaded[k % RING], 16)
                        sp.dma_start(ctx_raw[:, k % RING, TT:TT + TI], ipT[k * P:(k + 1) * P, :]).then_inc(ctx_loaded[k % RING], 16)
                        if k == RING - 1:
                            sp.dma_start(bias[:], b_out).then_inc(small_loaded, 16)
                            sp.dma_start(boxes[:].rearrange("p n f -> p (n f)"),
                                         bbox.rearrange("(o b) m f -> o (b m f)", o=1).broadcast_to([P, B * BOXES * 4])).then_inc(small_loaded, 16)
                            sp.dma_start(gx[:], grid_x).then_inc(small_loaded, 16)
                            sp.dma_start(gy[:], grid_y).then_inc(small_loaded, 16)
                    for c in range(KC, KC + LOADS + RING - 1):
                        load_chunk(c)
                    v_pairs = v_scratch.rearrange("(i j) k d -> j k i d", j=2)
                    sp.wait_ge(v_text_act, NPB)
                    sp.wait_ge(v_text_dve, NPB)
                    for j in range(2):
                        sp.dma_start(v_pairs[j, 0:NTEXT, :, :], v_text[j * NTEXT:(j + 1) * NTEXT, :, :]).then_inc(v_stored, 16)
                    for c in range(KC + LOADS + RING - 1, len(chunks)):
                        load_chunk(c)
                    sp.wait_ge(k_ipT_act, 1)
                    sp.wait_ge(k_text_act, (KD + 1) // 2)
                    sp.wait_ge(k_text_dve, KD // 2)
                    sp.dma_start(k_scratch.rearrange("p b n -> p (b n)"), k_all[:].rearrange("p b m k -> p (b m k)")).then_inc(k_stored, 16)
                    sp.wait_ge(ip_added, 3)
                    for b in range(B):
                        sp.dma_start(v_scratch[b, NTEXT:KEYS, :], v_ip[b * NIP:(b + 1) * NIP, :]).then_inc(v_stored, 16)
                    sp.wait_ge(k_stored, 16)
                    load_k(sp, 0)
                    sp.wait_ge(v_stored, 16 * (2 + B))

                @block.gpsimd
                def _(pool):
                    nc.gpsimd.memset(ident[:], 0.0).then_inc(ident_zeroed, 1)
                    pool.wait_ge(ident_zeroed, 1)
                    nc.gpsimd.affine_select(out=ident[:], in_=ident[:], compare_op=ALU.not_equal, fill=1.0, base=0,
                                            pattern=[[-1, P]], channel_multiplier=1).then_inc(ident_made, 1)
                    for buf in (k_hi, k_lo):
                        nc.gpsimd.memset(buf[:].rearrange("p m j k -> p (m j k)").bitcast(F32), 0.0).then_inc(k_zeroed, 1)
                    for c in range(1, len(chunks), 2):
                        hi, lo = split_dst(c)
                        pool.wait_ge(w_hi_done, c + 1)
                        nc.gpsimd.tensor_tensor(lo, w_raw[:, c % LOADS, :], hi.bitcast(F32), ALU.subtract).then_inc(w_lo_done[1], 1)

                @block.scalar
                def _(act):
                    def round_chunk(c):
                        act.wait_ge(w_loaded[c % LOADS], 16 * (c // LOADS + 1))
                        r = ring_place[c]
                        if r is not None and r >= RING:
                            r -= RING
                            if r < KC - 1:
                                act.wait_ge(w_used, r + 1)
                            elif r == KC - 1:
                                act.wait_ge(v_text_ready, 2 * NPB)
                            else:
                                k, of_ip = divmod(r - KC, 3)
                                act.wait_ge(w_used, KC - 1 + 3 * k + (3 if of_ip else 1))
                        nc.scalar.activation(split_dst(c)[0], w_raw[:, c % LOADS, :], ACT.Copy).then_inc(w_hi_done, 1)

                    for k in range(KC):
                        round_chunk(k)
                        act.wait_ge(ctx_loaded[k % RING], 32 * (k // RING + 1))
                        nc.scalar.activation(ctxT_hi[:, k, :], ctx_raw[:, k % RING, 0:TT], ACT.Copy)
                        nc.scalar.activation(ipT_parts[:, k, 0, :], ctx_raw[:, k % RING, TT:TT + TI], ACT.Copy).then_inc(ctx_hi_done, 1)
                    for c in range(KC, KC + RING - 1):
                        round_chunk(c)
                    act.dma_start(xin[:, 0, :, :], x_half[0, 0]).then_inc(x_loaded[0], 16)
                    for i in range(NPB):
                        act.wait_ge(v_text_ready, 2 * i + 1)
                        nc.scalar.activation(v_text[:, i, 0:HALF], bank[2 * i][0:PB, 0:HALF], ACT.Copy).then_inc(v_text_act, 1)
                    for c in range(KC + RING - 1, WO0):
                        round_chunk(c)
                        if chunks[c][0] == "q":
                            if chunks[c][1] == 0:
                                act.wait_ge(x_loaded[0], 16)
                            x_hi_part(act, 0, 0, chunks[c][1])
                    for n, (i, c0, c1) in enumerate(IP_BANKS):
                        act.wait_ge(ip_ready, n + 1)
                        nc.scalar.activation(ip_part[:, c0:c1], bank[i][TI:P, 0:c1 - c0], ACT.Copy).then_inc(ip_moved, 1)
                    for m in reversed(range(0, KD, 2)):
                        act.wait_ge(k_text_ready, KD)
                        nc.scalar.activation(k_all[:, :, m, 0:NTEXT], bank[2 + m][:, 0:TT].rearrange("p (b k) -> p b k", b=B),
                                             ACT.Copy, scale=SCALE).then_inc(k_text_act, 1)
                    act.wait_ge(k_ipT_ready, 1)
                    nc.scalar.activation(k_all[:, :, :, NTEXT:KEYS].rearrange("p b m k -> p m b k"),
                                         bank[1][:, 0:KD * TI].rearrange("p (m b k) -> p m b k", b=B, k=NIP), ACT.Copy, scale=SCALE).then_inc(k_ipT_act, 1)
                    act.dma_start(xin[:, 1, :, :], x_half[1, 0]).then_inc(x_loaded[1], 16)
                    for m in range(KD):
                        round_chunk(WO0 + m)
                        if m < KD - 1:
                            q_hi_part(act, 0, m)
                        if m == KD - 3:
                            act.wait_ge(k_zeroed, 2)
                            k_hi_part(act, 0)

                @block.vector
                def _(dve):
                    def lo_chunk(c):
                        if c % 2 == 0:
                            hi, lo = split_dst(c)
                            dve.wait_ge(w_hi_done, c + 1)
                            nc.vector.tensor_tensor(lo, w_raw[:, c % LOADS, :], hi.bitcast(F32), ALU.subtract).then_inc(w_lo_done[0], 1)

                    def make_mask():
                        steps = [0]

                        def step(ins):
                            ins.then_inc(mask_step, 1)
                            steps[0] += 1
                            dve.wait_ge(mask_step, steps[0])

                        def edge(f, cols=None):
                            e = boxes[:, :, f]
                            return e if cols is None else e.unsqueeze(2).broadcast_to([P, B * BOXES, cols])

                        dve.wait_ge(small_loaded, 64)
                        y_all = gy[:].unsqueeze(1).broadcast_to([P, B * BOXES, TPB])
                        nc.vector.tensor_scalar(inside_x[:, 0, :], edge(0), gx[:, 0:1], None, ALU.is_le)
                        nc.vector.tensor_scalar(inside_x[:, 1, :], edge(2), gx[:, 0:1], None, ALU.is_ge)
                        nc.vector.tensor_tensor(inside_y[:, 0, :, :], y_all, edge(1, TPB), ALU.is_ge)
                        step(nc.vector.tensor_tensor(inside_y[:, 1, :, :], y_all, edge(3, TPB), ALU.is_le))
                        step(nc.vector.tensor_tensor(inside_x[:, 0, :], inside_x[:, 0, :], inside_x[:, 1, :], ALU.mult))
                        step(nc.vector.tensor_tensor(inside_y[:, 0, :, :], inside_y[:, 0, :, :], inside_y[:, 1, :, :], ALU.mult))
                        ins_all = inside[:].rearrange("p b m t -> p (b m) t")
                        step(nc.vector.tensor_tensor(ins_all, inside_y[:, 0, :, :], inside_x[:, 0, :].unsqueeze(2).broadcast_to([P, B * BOXES, TPB]), ALU.mult))
                        step(nc.vector.tensor_reduce(any_in[:], inside[:].rearrange("p b m t -> p b t m"), AX.X, ALU.max))
                        mask_b = mask[:].rearrange("p (b t) k -> p b t k", b=B)
                        for n in range(BOXES):
                            nc.vector.tensor_scalar(mask_b[:, :, :, n], any_in[:], NEG, None, ALU.mult)
                            last = nc.vector.tensor_scalar(mask_b[:, :, :, BOXES + n], inside[:, :, n, :], 1.0, -NEG, ALU.subtract, ALU.mult)
                        step(last)

                    for k in range(KC):
                        lo_chunk(k)
                        dve.wait_ge(ctx_hi_done, k + 1)
                        nc.vector.tensor_tensor(ctxT_lo[:, k, :], ctx_raw[:, k % RING, 0:TT], ctxT_hi[:, k, :].bitcast(F32), ALU.subtract)
                        nc.vector.tensor_tensor(ipT_parts[:, k, 1, :], ctx_raw[:, k % RING, TT:TT + TI], ipT_parts[:, k, 0, :].bitcast(F32), ALU.subtract).then_inc(ctx_lo_done, 1)
                        if k == RING:
                            make_mask()
                    for c in range(KC, KC + RING - 1):
                        lo_chunk(c)
                    for i in range(NPB):
                        dve.wait_ge(v_text_ready, 2 * i + 2)
                        nc.vector.tensor_copy(v_text[:, i, HALF:D], bank[2 * i + 1][0:PB, 0:HALF]).then_inc(v_text_dve, 1)
                    for c in range(KC + RING - 1, WO0):
                        lo_chunk(c)
                        if chunks[c][0] == "q":
                            x_lo_part(dve, 0, 0, chunks[c][1])
                    for n, (i, c0, c1) in enumerate(IP_BANKS):
                        dve.wait_ge(ip_moved, n + 1)
                        if i == 7:
                            nc.vector.tensor_tensor(v_ip[:, 512:D], bank[i][0:TI, 0:REST], ip_part[:, c0:c0 + REST], ALU.add)
                            nc.vector.tensor_tensor(k_ip[:, 512:D], bank[i][0:TI, REST:2 * REST], ip_part[:, c0 + REST:c1], ALU.add).then_inc(ip_added, 1)
                        else:
                            nc.vector.tensor_tensor((k_ip if i else v_ip)[:, 0:512], bank[i][0:TI, 0:512], ip_part[:, c0:c1], ALU.add).then_inc(ip_added, 1)
                    for m in range(1, KD, 2):
                        dve.wait_ge(k_text_ready, m + 1)
                        nc.vector.tensor_scalar(k_all[:, :, m, 0:NTEXT], bank[2 + m][:, 0:TT].rearrange("p (b k) -> p b k", b=B),
                                                SCALE, None, ALU.mult).then_inc(k_text_dve, 1)
                    for m in range(KD):
                        lo_chunk(WO0 + m)
                        if m < KD - 1:
                            q_lo_part(dve, 0, m)
                        if m == KD - 3:
                            k_lo_part(dve, 0)

                @block.tensor
                def _(pe):
                    for k in range(KC):
                        pe.wait_ge(ctx_lo_done, k + 1)
                        wait_lo(pe, "v", k)
                        s = slot("v", k)
                        for n in range(2 * NPB):
                            toks, cols = slice(n // 2 * PB, (n // 2 + 1) * PB), slice(n % 2 * HALF, (n % 2 + 1) * HALF)
                            ins = three(bank[n][0:PB, 0:HALF], ctxT_hi[:, k, toks], ctxT_lo[:, k, toks], w_hi[:, s, cols], w_lo[:, s, cols],
                                        k == 0, k == KC - 1)
                            if k == KC - 1:
                                ins.then_inc(v_text_ready, 1)
                        if k < KC - 1:
                            ins.then_inc(w_used, 1)

                    def text_keys(k, tiles):
                        wait_lo(pe, "k", k)
                        s = slot("k", k)
                        for m in tiles:
                            if k == 0:
                                pe.wait_ge(v_text_dve if m % 2 else v_text_act, (2 + m) // 2 + 1)
                            rows = slice(m * P, (m + 1) * P)
                            ins = three(bank[2 + m][:, 0:TT], w_hi[:, s, rows], w_lo[:, s, rows], ctxT_hi[:, k, :], ctxT_lo[:, k, :], k == 0, k == KC - 1)
                            if k == KC - 1:
                                ins.then_inc(k_text_ready, 1)
                        if k < KC - 1:
                            ins.then_inc(w_used, 1)

                    def ip_keys_values(k):
                        wait_lo(pe, "v_ip", k)
                        wait_lo(pe, "k_ip", k)
                        sv, sk = slot("v_ip", k), slot("k_ip", k)
                        toks = ipT_parts[:, k, :, :].rearrange("p s t -> p (s t)")
                        for i, c0, c1 in IP_BANKS:
                            if k == 0:
                                pe.wait_ge(v_text_dve if i % 2 else v_text_act, i // 2 + 1)
                            for part in (w_hi, w_lo):
                                if i == 7:
                                    dst = bank[i][:, 0:2 * REST].rearrange("p (w c) -> p w c", w=2)
                                    src = part[:, sv:sk + 1:sk - sv, 512:D]
                                else:
                                    dst, src = bank[i][:], part[:, sk if i else sv, 0:512]
                                ins = nc.tensor.matmul(dst, toks, src, start=k == 0 and part is w_hi, stop=k == KC - 1 and part is w_lo)
                            if k == KC - 1:
                                ins.then_inc(ip_ready, 1)
                        if k < KC - 1:
                            ins.then_inc(w_used, 2)

                    for k in range(KC - 1):
                        text_keys(k, range(KD))
                        ip_keys_values(k)
                    text_keys(KC - 1, range(3))
                    ip_keys_values(KC - 1)
                    text_keys(KC - 1, range(3, KD))
                    pe.wait_ge(ident_made, 1)
                    pe.wait_ge(ip_added, 2)
                    for m in range(KD):
                        ins = nc.tensor.transpose(bank[1][:, m * TI:(m + 1) * TI], k_ip[:, m * P:(m + 1) * P], ident[0:TI, 0:TI])
                    ins.then_inc(k_ipT_ready, 1)
                    for m in range(KD):
                        if m == 0:
                            for k in range(KD):
                                wait_lo(pe, "q", k)
                        elif m == 1:
                            pe.wait_ge(k_text_act, 1)
                        else:
                            pe.wait_ge(q_lo_done, m - 1)
                        q_steps(pe, 0, m)

        res = sb("res", [P, 2, KD, GQ])
        prob = sb("prob", [P, GT * SW])
        pT_hi, pT_lo = sb("pT_hi", [P, 2, GQ], F32R), sb("pT_lo", [P, 2, GQ], F32R)
        pv_part = sb("pv_part", [P, GQ])
        o_raw = sb("o_raw", [P, 2, GQ])
        oT_hi, oT_lo = sb("oT_hi", [P, KD, GQ], F32R), sb("oT_lo", [P, KD, GQ], F32R)
        v_raw = sb("v_raw", [P, D])
        v_parts = sb("v_parts", [P, PAIRS, 2, HP], F32R)
        top, total, inv = sb("top", [P, GT, 2, HEADS]), sb("total", [P, GT, 2, HEADS]), sb("inv", [P, GT, 2, HEADS])

        s_bank, t_bank, v_bank = bank[0:4], bank[2:4], bank[4:6]

        v_raw_loaded, v_zeroed, v_hi_built, v_built = (sem(n) for n in ("v_raw_loaded", "v_zeroed", "v_hi_built", "v_built"))
        score_ready, pT_ready, pv_ready, out_ready = (sem(n) for n in ("score_ready", "pT_ready", "pv_ready", "out_ready"))
        score_copied, exp_done, res_done, pT_hi_done, pv_moved, oT_hi_done = (
            sem(n) for n in ("score_copied", "exp_done", "res_done", "pT_hi_done", "pv_moved", "oT_hi_done"))
        max_done, sum_done, inv_done, pT_lo_done, pv_added, out_done = (
            sem(n) for n in ("max_done", "sum_done", "inv_done", "pT_lo_done", "pv_added", "out_done"))
        mask_added, max_subbed, prob_done, oT_lo_done = (sem(n) for n in ("mask_added", "max_subbed", "prob_done", "oT_lo_done"))
        last_max_subbed, last_prob_done = sem("last_max_subbed"), sem("last_prob_done")
        stored = [sem("stored0"), sem("stored1")]

        def units_for_tile(t):
            return -(-(t + 1) * SW // 512)

        def tile(t):
            return prob[:, t * SW:(t + 1) * SW].rearrange("p (h k) -> p h k", k=KEYS)

        def own_rows(p):
            return (slice(0, HP), slice(HP, P)) if p % 2 == 0 else (slice(HP, P), slice(0, HP))

        def q_ahead(before):
            return 2 if before else KD

        def q_slot(s, before):
            rest = KD - q_ahead(before)
            return [(q_ahead(before) + i // KD, i % KD) for i in range(s * rest, (s + 1) * rest)]

        def q_finished(s, before):
            return [m for m, k in q_slot(s, before) if k == KD - 1]

        def v_head(t, part, j):
            return t[j * HP:(j + 1) * HP, :, part, j * DH:(j + 1) * DH]

        def v_own(j):
            return v_raw[j * HP:(j + 1) * HP, :].rearrange("p (n c) -> p n c", n=PAIRS)[:, :, j * DH:(j + 1) * DH]

        SPANS = ((0, NTEXT), (NTEXT, KEYS))

        def turns(shared):
            return (0, 1, 3, 2) if shared else (0, 1, 2, 3)

        def subtract_top(eng, t):
            for n, (k0, k1) in enumerate(SPANS):
                s = tile(t)[:, :, k0:k1]
                ins = eng.tensor_tensor(s, s, top[:, t, n, :].unsqueeze(2).broadcast_to([P, HEADS, k1 - k0]), ALU.subtract)
            return ins

        def scale_by_inv(eng, t):
            for n, (k0, k1) in enumerate(SPANS):
                s = tile(t)[:, :, k0:k1]
                ins = eng.tensor_tensor(s, s, inv[:, t, n, :].unsqueeze(2).broadcast_to([P, HEADS, k1 - k0]), ALU.mult)
            return ins

        with nc.Block() as block:

            @block.sync
            def _(sp):
                def load_v(b):
                    wait(sp, v_built, 2 * b)
                    for h in range(2):
                        sp.dma_start(v_raw[h * KEYS:(h + 1) * KEYS, :], v_scratch[b]).then_inc(v_raw_loaded, 16)

                def group(g, u, b, stores, loads):
                    if loads and u == 0:
                        sp.wait_ge(k_built, HPT * (b + 1))
                        load_k(sp, b + 1)
                    if loads and u == 1:
                        load_v(b + 1)
                    if loads:
                        sp.wait_ge(res_done, KD * (g + 1))
                        sp.wait_ge(xT_lo_done, KD * (g + 1))
                        sp.dma_start(xin[:, u, :, :], x_half[u, b + 1]).then_inc(x_loaded[u], 16)
                    if stores:
                        for m in range(KD):
                            store(g - 1, 1 - u, b if u else b - 1, m)

                def store(g, u, b, m):
                    sp.wait_ge(out_done, KD * g + m + 1)
                    sp.dma_start(out_half[u, b, m], res[:, u, m, :]).then_inc(stored[u], 16)

                load_v(0)
                group(0, 0, 0, False, True)
                group(1, 1, 0, True, True)
                with sp.Fori(1, B - 1) as b:
                    group(2 * b, 0, b, True, True)
                    group(2 * b + 1, 1, b, True, True)
                group(NG - 2, 0, B - 1, True, False)
                group(NG - 1, 1, B - 1, True, False)
                for m in range(KD):
                    store(NG - 1, 1, B - 1, m)
                for u in range(2):
                    sp.wait_ge(stored[u], 16 * KD * NG // 2)

            @block.gpsimd
            def _(pool):
                def add_mask(g, t):
                    pool.wait_ge(score_copied, UNITS * g + units_for_tile(t))
                    ip = tile(t)[:, :, NTEXT:KEYS]
                    m = mask[:, GT * g + t, :].unsqueeze(1).broadcast_to([P, HEADS, NIP])
                    nc.gpsimd.tensor_tensor(ip, ip, m, ALU.add).then_inc(mask_added, 1)

                def sub_max(g, t, count):
                    pool.wait_ge(max_done, GT * g + t + 1)
                    subtract_top(nc.gpsimd, t).then_inc(max_subbed, count)

                def normalise(g, t, shared, count):
                    pool.wait_ge(inv_done, GT * g + turns(shared).index(t) + 1)
                    scale_by_inv(nc.gpsimd, t).then_inc(prob_done, count)

                def oT_part(g, m):
                    pool.wait_ge(oT_hi_done, KD * g + m + 1)
                    nc.gpsimd.tensor_tensor(oT_lo[:, m, :], o_raw[:, m % 2, :], oT_hi[:, m, :].bitcast(F32), ALU.subtract).then_inc(oT_lo_done, 1)

                def group(g, before, shared=0):
                    tiles = [(t, 1) for t in range(GT)] if not shared else [(t, 1 + t // (GT - 2)) for t in range(GT - 1)]
                    add_mask(g, 0)
                    if before:
                        oT_part(g - 1, KD - 1)
                    add_mask(g, 1)
                    add_mask(g, 2)
                    for t, count in tiles:
                        sub_max(g, t, count)
                        if t == 0:
                            add_mask(g, 3)
                    for t, count in tiles:
                        normalise(g, t, shared, count)
                    for m in range(KD - 1):
                        oT_part(g, m)

                nc.gpsimd.memset(v_parts[:].rearrange("p n s c -> p (n s c)").bitcast(F32), 0.0).then_inc(v_zeroed, 1)
                group(0, False, 1)
                group(1, True)
                with pool.Fori(1, B - 1) as b:
                    group(2 * b, True)
                    group(2 * b + 1, True)
                group(NG - 2, True)
                group(NG - 1, True, 2)
                oT_part(NG - 1, KD - 1)

            @block.scalar
            def _(act):
                def copy_scores(g, u):
                    act.wait_ge(score_ready, UNITS * g + u + 1)
                    nc.scalar.activation(prob[:, u * 512:(u + 1) * 512], s_bank[u % 4][:], ACT.Copy).then_inc(score_copied, 1)

                def exponentials(g, t, shared):
                    if shared and t == GT - 1:
                        act.wait_ge(last_max_subbed, shared)
                    else:
                        act.wait_ge(max_subbed, GT * g + t + 1)
                    nc.scalar.activation(prob[:, t * SW:(t + 1) * SW], prob[:, t * SW:(t + 1) * SW], ACT.Exp).then_inc(exp_done, 1)

                def pT_part(g, p):
                    act.wait_ge(pT_ready, PAIRS * g + p + 1)
                    nc.scalar.activation(pT_hi[:, p % 2, :], t_bank[p % 2][:], ACT.Copy).then_inc(pT_hi_done, 1)

                def move_pv(g, p):
                    act.wait_ge(pv_ready, PAIRS * g + p + 1)
                    own, other = own_rows(p)
                    nc.scalar.activation(pv_part[own, :], v_bank[p % 2][other, :], ACT.Copy).then_inc(pv_moved, 1)

                def oT_part(g, m):
                    act.wait_ge(pv_added, PAIRS * g + 2 * m + 2)
                    nc.scalar.activation(oT_hi[:, m, :], o_raw[:, m % 2, :], ACT.Copy).then_inc(oT_hi_done, 1)

                def residual(g, u, b, m):
                    if m == 0:
                        wait(act, x_loaded[u], 16 * (b + 1))
                        wait(act, stored[u], 16 * KD * b)
                    nc.scalar.activation(res[:, u, m, :], xin[:, u, m, :], ACT.Identity, bias=bias[:, m:m + 1]).then_inc(res_done, 1)

                def v_hi_part(b):
                    act.wait_ge(v_zeroed, 1)
                    act.wait_ge(v_raw_loaded, 32 * (b + 1))
                    wait(act, pv_ready, PAIRS * GPB * b)
                    for j in range(2):
                        nc.scalar.activation(v_head(v_parts, 0, j), v_own(j), ACT.Copy).then_inc(v_hi_built, 1)

                def group(g, u, b, before, more, shared=0):
                    def split_x(k0, k1):
                        if more:
                            if k0 == 0:
                                act.wait_ge(x_loaded[1 - u], 16 * (b + u + 1))
                                act.wait_ge(q_ready, KD * (g + 1))
                            for k in range(k0, k1):
                                x_hi_part(act, g + 1, 1 - u, k)

                    if not before:
                        split_x(0, KD)
                    for n in range(UNITS):
                        copy_scores(g, n)
                        if n == 1 and before:
                            oT_part(g - 1, KD - 1)
                    if before:
                        split_x(0, 3)
                    for n, t in enumerate(turns(shared)):
                        exponentials(g, t, shared)
                        if before and n == 0:
                            split_x(3, KD)
                        if not before and n < 3:
                            q_hi_part(act, g + 1, n)
                    for m in range(KD):
                        residual(g, u, b, m)
                    if u == 0:
                        v_hi_part(b)
                    elif more:
                        act.wait_ge(score_ready, UNITS * (g + 1))
                        k_hi_part(act, b + 1)
                    if more:
                        for m in range(0 if before else 3, q_ahead(before)):
                            q_hi_part(act, g + 1, m)
                    pT_part(g, 0)
                    pT_part(g, 1)
                    for s in range(KD):
                        if s:
                            oT_part(g, s - 1)
                        if more:
                            for m in q_finished(s, before):
                                q_hi_part(act, g + 1, m)
                        for p in (2 * s, 2 * s + 1):
                            move_pv(g, p)
                            if p + 2 < PAIRS:
                                pT_part(g, p + 2)

                q_hi_part(act, 0, KD - 1)
                group(0, 0, 0, False, True, 1)
                group(1, 1, 0, True, True)
                with act.Fori(1, B - 1) as b:
                    group(2 * b, 0, b, True, True)
                    group(2 * b + 1, 1, b, True, True)
                group(NG - 2, 0, B - 1, True, True)
                group(NG - 1, 1, B - 1, True, False, 2)
                oT_part(NG - 1, KD - 1)

            @block.vector
            def _(dve):
                def pT_part(g, p):
                    dve.wait_ge(pT_hi_done, PAIRS * g + p + 1)
                    nc.vector.tensor_tensor(pT_lo[:, p % 2, :], t_bank[p % 2][:], pT_hi[:, p % 2, :].bitcast(F32), ALU.subtract).then_inc(pT_lo_done, 1)

                def add_pv(g, p):
                    m, own = p // 2, own_rows(p)[0]
                    if p % 2 == 0:
                        wait(dve, oT_lo_done, KD * g + max(m - 1, 0))
                    dve.wait_ge(pv_moved, PAIRS * g + p + 1)
                    nc.vector.tensor_tensor(o_raw[own, m % 2, :], v_bank[p % 2][own, :], pv_part[own, :], ALU.add).then_inc(pv_added, 1)

                def maxima(g, t):
                    dve.wait_ge(mask_added, GT * g + t + 1)
                    for n, (k0, k1) in enumerate(SPANS):
                        ins = nc.vector.tensor_reduce(top[:, t, n, :], tile(t)[:, :, k0:k1], AX.X, ALU.max)
                    ins.then_inc(max_done, 1)

                def sums(g, t, n):
                    dve.wait_ge(exp_done, GT * g + n + 1)
                    for span, (k0, k1) in enumerate(SPANS):
                        nc.vector.tensor_reduce(total[:, t, span, :], tile(t)[:, :, k0:k1], AX.X, ALU.add).then_inc(sum_done, 1)
                    dve.wait_ge(sum_done, 2 * (GT * g + n + 1))
                    nc.vector.reciprocal(inv[:, t, :, :], total[:, t, :, :]).then_inc(inv_done, 1)

                def output(g, u, m):
                    if m == 0:
                        dve.wait_ge(res_done, KD * (g + 1))
                    dve.wait_ge(out_ready, KD * g + m + 1)
                    r = res[:, u, m, :]
                    nc.vector.tensor_tensor(r, l_bank[m % 2][:], r, ALU.add).then_inc(out_done, 1)

                def v_lo_part(b):
                    for j in range(2):
                        dve.wait_ge(v_hi_built, 2 * b + j + 1)
                        nc.vector.tensor_tensor(v_head(v_parts, 1, j), v_own(j), v_head(v_parts, 0, j).bitcast(F32), ALU.subtract).then_inc(v_built, 1)

                def group(g, u, b, before, more, shared=0):
                    def split_x(k0, k1):
                        if more:
                            for k in range(k0, k1):
                                x_lo_part(dve, g + 1, 1 - u, k)

                    if not before:
                        split_x(0, KD)
                    for t in range(GT):
                        maxima(g, t)
                        if before and t == 2:
                            split_x(0, 2)
                    if not before:
                        q_lo_part(dve, g + 1, 0)
                    if shared:
                        dve.wait_ge(max_done, GT * (g + 1))
                        subtract_top(nc.vector, GT - 1).then_inc(last_max_subbed, 1)
                    if before:
                        output(g - 1, 1 - u, 0)
                    for n, t in enumerate(turns(shared)):
                        if before and n < 3:
                            split_x(n + 2, n + 3)
                        sums(g, t, n)
                        if shared and n == 3:
                            dve.wait_ge(inv_done, GT * (g + 1) - 1)
                            scale_by_inv(nc.vector, GT - 1).then_inc(last_prob_done, 1)
                        if before:
                            output(g - 1, 1 - u, n + 1)
                        elif n == 1 or n == 2:
                            q_lo_part(dve, g + 1, n)
                    if u == 0:
                        v_lo_part(b)
                    elif more:
                        k_lo_part(dve, b + 1)
                    if more:
                        for m in range(0 if before else 3, q_ahead(before)):
                            q_lo_part(dve, g + 1, m)
                    pT_part(g, 0)
                    pT_part(g, 1)
                    for s in range(KD):
                        if more:
                            for m in q_finished(s, before):
                                q_lo_part(dve, g + 1, m)
                        for p in (2 * s, 2 * s + 1):
                            add_pv(g, p)
                            if p + 2 < PAIRS:
                                pT_part(g, p + 2)

                q_lo_part(dve, 0, KD - 1)
                group(0, 0, 0, False, True, 1)
                group(1, 1, 0, True, True)
                with dve.Fori(1, B - 1) as b:
                    group(2 * b, 0, b, True, True)
                    group(2 * b + 1, 1, b, True, True)
                group(NG - 2, 0, B - 1, True, True)
                group(NG - 1, 1, B - 1, True, False, 2)
                for m in range(KD):
                    output(NG - 1, 1, m)

            @block.tensor
            def _(pe):
                def score_unit(g, n, b, new_batch):
                    if n < 2:
                        wait(pe, score_copied, UNITS * g)
                    elif n < 4:
                        wait(pe, pT_lo_done, PAIRS * g)
                    else:
                        pe.wait_ge(score_copied, UNITS * g + n - 3)
                    if n == 0 and new_batch:
                        pe.wait_ge(k_built, HPT * (b + 1))
                    for half in range(2):
                        t, m = divmod(2 * n + half, KD)
                        if t == 0:
                            pe.wait_ge(q_lo_done, KD * g + m + 1)
                        q_cols = slice(t * P, (t + 1) * P)
                        keys = [k[:, m, :, :].rearrange("p j k -> p (j k)") for k in (k_hi, k_lo)]
                        ins = three(s_bank[n % 4][:, half * CW:(half + 1) * CW], qT_hi[:, m, q_cols], qT_lo[:, m, q_cols], *keys, True, True)
                    ins.then_inc(score_ready, 1)

                def p_transpose(g, p, shared):
                    if p < 2:
                        pe.wait_ge(score_copied, UNITS * (g + 1))
                    else:
                        pe.wait_ge(pT_lo_done, PAIRS * g + p - 1)
                    for t in range(GT):
                        if p == 0 and shared and t == GT - 1:
                            pe.wait_ge(last_prob_done, shared)
                        elif p == 0:
                            pe.wait_ge(prob_done, GT * g + t + 1)
                        src = prob[:, t * SW + p * P:t * SW + (p + 1) * P]
                        ins = nc.tensor.transpose(t_bank[p % 2][:, t * P:(t + 1) * P], src, ident[:])
                    ins.then_inc(pT_ready, 1)

                def pv_pair(g, p, b, new_batch):
                    if p == 0 and new_batch:
                        pe.wait_ge(v_built, 2 * (b + 1))
                    wait(pe, pv_added, PAIRS * g + max(p - 1, 0))
                    pe.wait_ge(pT_lo_done, PAIRS * g + p + 1)
                    v = v_parts[:, p, :, :].rearrange("p s c -> p (s c)")
                    nc.tensor.matmul(v_bank[p % 2][:], v, pT_hi[:, p % 2, :], start=True, stop=False)
                    nc.tensor.matmul(v_bank[p % 2][:], v, pT_lo[:, p % 2, :], start=False, stop=True).then_inc(pv_ready, 1)

                def out_tile(g, m, more=True):
                    if m >= 2:
                        pe.wait_ge(out_done, KD * g + m - 1)
                    elif more:
                        pe.wait_ge(q_lo_done, KD * (g + 2))
                    else:
                        pe.wait_ge(out_done, KD * g)
                    cols = slice(m * P, (m + 1) * P)
                    for k in range(KD):
                        if m == 0:
                            pe.wait_ge(oT_lo_done, KD * g + k + 1)
                        ins = three(l_bank[m % 2][:], wo_hi[:, k, cols], wo_lo[:, k, cols], oT_hi[:, k, :], oT_lo[:, k, :], k == 0, k == KD - 1)
                    ins.then_inc(out_ready, 1)

                def group(g, b, new_batch, before, more, shared=0):
                    for n in range(UNITS):
                        score_unit(g, n, b, new_batch)
                    if before:
                        for m in range(KD):
                            out_tile(g - 1, m)
                    if more:
                        for m in range(q_ahead(before)):
                            if m < 2:
                                wait(pe, out_done, KD * g - (1 if m == 0 else 0))
                            else:
                                pe.wait_ge(q_lo_done, KD * (g + 1) + m - 1)
                            q_steps(pe, g + 1, m)
                    p_transpose(g, 0, shared)
                    p_transpose(g, 1, shared)
                    for s in range(KD):
                        if more:
                            for m, k in q_slot(s, before):
                                if k == 0:
                                    pe.wait_ge(q_lo_done, KD * (g + 1) + m - 1)
                                q_steps(pe, g + 1, m, k, k + 1)
                        for p in (2 * s, 2 * s + 1):
                            pv_pair(g, p, b, new_batch)
                            if p + 2 < PAIRS:
                                p_transpose(g, p + 2, shared)

                group(0, 0, True, False, True, 1)
                group(1, 0, False, True, True)
                with pe.Fori(1, B - 1) as b:
                    group(2 * b, b, True, True, True)
                    group(2 * b + 1, b, False, True, True)
                group(NG - 2, B - 1, True, True, True)
                group(NG - 1, B - 1, False, True, False, 2)
                for m in range(KD):
                    out_tile(NG - 1, m, more=False)


_WEIGHTS = ["L0_xattn_w_q", "L0_xattn_w_k", "L0_xattn_w_v", "L0_xattn_w_k_ip", "L0_xattn_w_v_ip", "L0_xattn_w_out"]


def kernel(**inputs):
    import numpy as np
    import concourse.bacc as bacc
    from concourse.bass_utils import run_bass_kernel_spmd

    x, ctx = np.asarray(inputs["x"]), np.asarray(inputs["ctx_2048"])
    width, seq = ctx.shape[2], x.shape[1]
    text = ctx.shape[1] - NIP
    line = np.arange(GRID, dtype=np.float32) * np.float32(1.0 / (GRID - 1))
    n = np.arange(seq).reshape(seq // P, P).T
    laid_out = {
        "xT": x.transpose(0, 2, 1),
        "textT": ctx[:, :text].transpose(2, 0, 1).reshape(width, -1),
        "ipT": ctx[:, text:].transpose(2, 0, 1).reshape(width, -1),
        "bbox": np.asarray(inputs["fside_Bx4x4_0"]),
        **{w: np.asarray(inputs[w]) for w in _WEIGHTS},
        "b_out": np.asarray(inputs["L0_xattn_b_out"]).reshape(-1, P).T,
        "grid_x": line[n[:, 0:1] % GRID],
        "grid_y": line[n // GRID],
    }
    nc = bacc.Bacc("TRN2", target_bir_lowering=False, num_devices=1)
    arrays, args = {}, []
    for name, a in laid_out.items():
        a = np.ascontiguousarray(a)
        arrays[f"in_{name}"] = a
        args.append(nc.dram_tensor(f"in_{name}", a.shape, mybir.dt.from_np(a.dtype), kind="ExternalInput").ap())
    args.append(nc.dram_tensor("outT", (x.shape[0], x.shape[2], x.shape[1]), F32, kind="ExternalOutput").ap())
    attention_kernel(nc, *args)
    r = run_bass_kernel_spmd(nc, [arrays], core_ids=[0])
    return np.ascontiguousarray(r.results[0]["outT"].transpose(0, 2, 1))
```
